# Optimizing a Trainium2 kernel written in Bass

```python
import numpy as np
import jax
import jax.numpy as jnp

def _softmax(x, axis=-1):
    return jax.nn.softmax(x, axis=axis)

def _gelu(x):
    return jax.nn.gelu(x, approximate=True)

def _silu(x):
    return jax.nn.silu(x)

def _sigmoid(x):
    return jax.nn.sigmoid(x)

def _layernorm(x, axis=-1, eps=1e-05):
    m = jnp.mean(x, axis=axis, keepdims=True)
    v = jnp.var(x, axis=axis, keepdims=True)
    return (x - m) / jnp.sqrt(v + eps)

def _scatter_add(tgt, idx, src, axis=0):
    return tgt.at[idx].add(src)

def _segment_sum(src, seg, n):
    return jax.ops.segment_sum(src, seg, n)
kernel_name = 'mk_adj_preln_d4_adj_r2_496129'

def setup_inputs(seed: int=0):
    np.random.seed(seed)
    _w = jnp.asarray

    def _rec_inputs():
        import jax
        import jax.numpy as jnp
        _gk = jax.random.key(seed)
        x = -0.000929 + 1 * jax.random.normal(jax.random.fold_in(_gk, 1), (8, 1024, 128), jnp.float32)
        _w = (1.0 + jnp.arange(1024, dtype=jnp.float32)) ** (-0.5)
        _w = _w / _w.mean()
        _pij = jnp.clip(0.015625 * _w[:, None] * _w[None, :], 0.0, 1.0)
        _a = jax.random.uniform(jax.random.fold_in(_gk, 2), (8, 1024, 1024)) < _pij
        _a = jnp.logical_or(_a, jnp.eye(1024, dtype=bool))
        adj = _a.astype(jnp.int32)
        return (x, adj)
    x, adj = _rec_inputs()

    def _L0_gnn_setup():
        import jax, jax.numpy as jnp
        import numpy as np
        B, N, D, T = (32, 128, 128, 8)
        NEG_SLOPE = 0.2
        key = jax.random.key(seed)
        ks = jax.random.split(key, 12)

        def xavier(k, shape, gain=1.0):
            fan_in, fan_out = (shape[0], shape[1])
            a = gain * np.sqrt(6.0 / (fan_in + fan_out))
            return jax.random.uniform(k, shape, jnp.float32, -a, a)
        return {'atom_embeddings': jax.random.normal(ks[0], (B, N, D), jnp.float32), 'edges': jax.random.randint(ks[1], (B, N, N), 0, T, jnp.int64), 'a': xavier(ks[2], (D, D * T), 1.414).reshape(D, D, T), 'qw': xavier(ks[3], (D, D)), 'qb': jnp.zeros((D,), jnp.float32), 'kw': xavier(ks[4], (D, D)), 'kb': jnp.zeros((D,), jnp.float32), 'vw': xavier(ks[5], (D, D)), 'vb': jnp.zeros((D,), jnp.float32), 'pw': xavier(ks[6], (D, D)), 'pb': jnp.zeros((D,), jnp.float32)}
    _L0_gnn_all = _L0_gnn_setup()
    _L0_gnn_in = {k: v for k, v in _L0_gnn_all.items() if k in ('a', 'qw', 'qb', 'kw', 'kb', 'vw', 'vb', 'pw', 'pb')}
    del _L0_gnn_all

    def _L1_gnn_setup():
        import jax, jax.numpy as jnp
        import numpy as np
        BATCH, SEQ, D_IN, D_OUT = (32, 512, 128, 128)
        NEG_SLOPE = 0.1
        key = jax.random.key(seed)
        k1, k2, k3, k4 = jax.random.split(key, 4)
        nodes = jax.random.normal(k1, (BATCH, SEQ, D_IN), dtype=jnp.float32)
        adjacent = jax.random.randint(k2, (BATCH, SEQ, SEQ), 0, 2, dtype=jnp.int32)
        W = jax.random.normal(k3, (D_IN, D_OUT), dtype=jnp.float32) / np.sqrt(D_IN)
        B = jax.random.normal(k4, (D_IN, D_OUT), dtype=jnp.float32) / np.sqrt(D_IN)
        return {'nodes': nodes, 'adjacent': adjacent, 'W': W, 'B': B}
    _L1_gnn_all = _L1_gnn_setup()
    _L1_gnn_in = {k: v for k, v in _L1_gnn_all.items() if k in ('W', 'B')}
    del _L1_gnn_all

    def _L2_gnn_setup():
        import jax, jax.numpy as jnp
        import numpy as np
        ALPHA = 0.2
        key = jax.random.key(seed)
        k1, k2, k3, k4 = jax.random.split(key, 4)
        B, N, D_in, D_out = (8, 1024, 128, 128)
        h = jax.random.normal(k1, (B, N, D_in), dtype=jnp.float32)
        adj = jax.random.randint(k2, (B, N, N), 0, 2, dtype=jnp.int32)
        W = jax.random.normal(k3, (D_in, D_out), dtype=jnp.float32) / np.sqrt(D_in)
        a = jax.random.normal(k4, (2 * D_out,), dtype=jnp.float32) / np.sqrt(2 * D_out)
        return {'h': h, 'adj': adj, 'W': W, 'a': a}
    _L2_gnn_all = _L2_gnn_setup()
    _L2_gnn_in = {k: v for k, v in _L2_gnn_all.items() if k in ('W', 'a')}
    del _L2_gnn_all

    def _L3_gnn_setup():
        import jax, jax.numpy as jnp
        import numpy as np
        B, N, D = (256, 64, 128)
        NEG = -9000000000000000.0
        key = jax.random.key(seed)
        k1, k2, k3 = jax.random.split(key, 3)
        hidden = jax.random.normal(k1, (B, N, D), dtype=jnp.float32)
        adj = jax.random.randint(k2, (B, N, N), 0, 5)
        A = jax.random.normal(k3, (4, D), dtype=jnp.float32) * 0.1
        return {'hidden': hidden, 'adj': adj, 'A': A}
    _L3_gnn_all = _L3_gnn_setup()
    _L3_gnn_in = {k: v for k, v in _L3_gnn_all.items() if k in ('A',)}
    del _L3_gnn_all
    return {'x': x, 'adj': adj, 'L0_gnn_a': _L0_gnn_in['a'], 'L0_gnn_qw': _L0_gnn_in['qw'], 'L0_gnn_qb': _L0_gnn_in['qb'], 'L0_gnn_kw': _L0_gnn_in['kw'], 'L0_gnn_kb': _L0_gnn_in['kb'], 'L0_gnn_vw': _L0_gnn_in['vw'], 'L0_gnn_vb': _L0_gnn_in['vb'], 'L0_gnn_pw': _L0_gnn_in['pw'], 'L0_gnn_pb': _L0_gnn_in['pb'], 'L1_gnn_W': _L1_gnn_in['W'], 'L1_gnn_B': _L1_gnn_in['B'], 'L2_gnn_W': _L2_gnn_in['W'], 'L2_gnn_a': _L2_gnn_in['a'], 'L3_gnn_A': _L3_gnn_in['A']}

def reference(x, adj, L0_gnn_a, L0_gnn_qw, L0_gnn_qb, L0_gnn_kw, L0_gnn_kb, L0_gnn_vw, L0_gnn_vb, L0_gnn_pw, L0_gnn_pb, L1_gnn_W, L1_gnn_B, L2_gnn_W, L2_gnn_a, L3_gnn_A):
    import jax
    import jax.numpy as jnp

    def _L0_gnn_ref(atom_embeddings, edges, a, qw, qb, kw, kb, vw, vb, pw, pb):
        import jax, jax.numpy as jnp
        import numpy as np
        B, N, D, T = (32, 128, 128, 8)
        NEG_SLOPE = 0.2
        x = atom_embeddings
        src = x @ qw.T + qb
        dst = x @ kw.T + kb
        val = x @ vw.T + vb
        scores = jnp.einsum('bnd,det,bme->bnmt', src, a, dst)
        s = jnp.take_along_axis(scores, jnp.clip(edges, 0)[..., None], axis=-1)[..., 0]
        s = jnp.where(edges == -1, -jnp.inf, s)
        s = jax.nn.leaky_relu(s, NEG_SLOPE)
        att = jax.nn.softmax(s, axis=-1)
        out = att @ val
        return out @ pw.T + pb

    def _L1_gnn_ref(nodes, adjacent, W, B):
        import jax, jax.numpy as jnp
        import numpy as np
        BATCH, SEQ, D_IN, D_OUT = (32, 512, 128, 128)
        NEG_SLOPE = 0.1
        mask = (adjacent != 0).astype(nodes.dtype)
        counts = mask.sum(axis=1)
        pooled = jnp.einsum('boi,bod->bid', mask, nodes)
        pooled = jnp.where(counts[..., None] > 0, pooled / jnp.maximum(counts, 1.0)[..., None], jnp.zeros((), dtype=nodes.dtype))
        updated = nodes @ B + pooled @ W
        return jax.nn.leaky_relu(updated, negative_slope=NEG_SLOPE)

    def _L2_gnn_ref(h, adj, W, a):
        import jax, jax.numpy as jnp
        import numpy as np
        ALPHA = 0.2
        D_out = W.shape[1]
        Wh = jnp.einsum('bnd,de->bne', h, W)
        a_src, a_dst = (a[:D_out], a[D_out:])
        s_i = Wh @ a_src
        s_j = Wh @ a_dst
        e = jax.nn.leaky_relu(s_i[:, :, None] + s_j[:, None, :], negative_slope=ALPHA)
        e = jnp.where(adj == 0, -jnp.inf, e)
        attention = jax.nn.softmax(e, axis=-1)
        h_prime = jnp.einsum('bij,bjd->bid', attention, Wh)
        return h_prime

    def _L3_gnn_ref(hidden, adj, A):
        import jax, jax.numpy as jnp
        import numpy as np
        B, N, D = (256, 64, 128)
        NEG = -9000000000000000.0
        h = hidden
        e = jnp.einsum('bid,kd,bjd->kbij', h, A, h)
        e = jax.nn.leaky_relu(e, negative_slope=0.2)
        alpha = jnp.full(adj.shape, jnp.float32(NEG), dtype=h.dtype)
        for t in range(4):
            alpha = jnp.where(adj == t + 1, e[t], alpha)
        alpha = jax.nn.softmax(alpha, axis=-1)
        return jnp.einsum('bij,bjd->bid', alpha, h)
    h = jnp.maximum(_layernorm(x, axis=-1), 0.0)
    x = x + _L0_gnn_ref(h, adj, L0_gnn_a, L0_gnn_qw, L0_gnn_qb, L0_gnn_kw, L0_gnn_kb, L0_gnn_vw, L0_gnn_vb, L0_gnn_pw, L0_gnn_pb)
    h = jnp.maximum(_layernorm(x, axis=-1), 0.0)
    x = x + _L1_gnn_ref(h, adj, L1_gnn_W, L1_gnn_B)
    h = jnp.maximum(_layernorm(x, axis=-1), 0.0)
    x = x + _L2_gnn_ref(h, adj, L2_gnn_W, L2_gnn_a)
    h = jnp.maximum(_layernorm(x, axis=-1), 0.0)
    x = x + _L3_gnn_ref(h, adj, L3_gnn_A)
    return x

_drawn_inputs = setup_inputs


def setup_inputs(seed=0):
    import zlib

    import numpy as np

    out = dict(_drawn_inputs(seed))
    spreads = {'L0_gnn_qb': (0.0, 0.1),
     'L0_gnn_kb': (0.0, 0.8),
     'L0_gnn_vb': (0.0, 0.1),
     'L0_gnn_pb': (0.0, 0.1)}
    factors = {}
    for name, (base, spread) in spreads.items():
        noise = np.random.default_rng([zlib.crc32(name.encode()), seed]).standard_normal(out[name].shape)
        drawn = base * np.exp(spread * noise) if base else spread * noise
        out[name] = jnp.asarray(drawn.astype(out[name].dtype))
    for name, factor in factors.items():
        out[name] = (out[name] * factor).astype(out[name].dtype)
    return out
```

```python
from contextlib import ExitStack, contextmanager, nullcontext

import concourse.bass as bass
from concourse import mybir

B, N, D, P = 8, 1024, 128, 128
R = N // P
HALF = N // 2
TYPES = 8
KINDS = 4
STAGE = 4
TURN_LAG, OUT_LAG = 1, 2
EPS = 1e-5
MASKED = -1.0e37
LOWEST = -3.0e38
LAYER3_NONE = -9.0e15
BITS_OF_1 = 0x3C00

ALU = mybir.AluOpType
ACT = mybir.ActivationFunctionType
AX = mybir.AxisListType
F32, F16, BF16 = mybir.dt.float32, mybir.dt.float16, mybir.dt.bfloat16
I32, I16, U16 = mybir.dt.int32, mybir.dt.int16, mybir.dt.uint16


def head_steps(layer, s, all_types):
    steps = [("stats", layer, s, 0), ("rstd", layer, s, 0), ("norm", layer, s, 0)]
    steps += [("turn_h", layer, s, c) for c in range(2)]
    if layer == 0:
        steps += [("dst", layer, s, c) for c in range(2)]
        steps += [("src", layer, s, 2 * t + c) for t in range(TYPES if all_types else 2) for c in range(2)]
        steps += [("val", layer, s, c) for c in range(2)]
    if layer == 1:
        steps += [("proj", layer, s, c) for c in range(4)]
        steps += [("pool", layer, s, c) for c in range(4)]
        steps += [("update", layer, s, 0)]
    if layer == 2:
        steps += [("wh", layer, s, c) for c in range(3)]
        steps += [("s_j", layer, s, c) for c in range(2)]
        steps += [("mask", layer, s, 0)]
    return steps


def schedule(all_types):
    if all_types:
        order, tile = [("fetch", 0)] + [("code", 0, r) for r in range(R)], 0
        for layer in (0, 1, 2, 3):
            order += [("light",) + st for st in head_steps(layer, 0, True)]
            if layer == 1:
                continue
            for t in range(R + OUT_LAG):
                if t < R:
                    order += [("front0", layer, 0, t, tile + t), ("front1", layer, 0, t, tile + t),
                              ("bias", layer, 0, t, tile + t)]
                if 0 <= t - TURN_LAG < R:
                    order += [("turn", tile + t - TURN_LAG)]
                if t < R:
                    order += [("exp", tile + t)]
                if 0 <= t - OUT_LAG < R:
                    order += [("out", layer, 0, t - OUT_LAG, tile + t - OUT_LAG)]
            tile += R
        return order + [("store", 0)]

    mid = lambda s: head_steps(1, s, False) + head_steps(2, s, False)
    phases = [((0, 0), head_steps(0, 1, False) + [("code", 1, r, 0) for r in range(R)]),
              ((0, 1), mid(0)), ((2, 0), mid(1)),
              ((2, 1), head_steps(3, 0, False) + [("code", 0, r, 0) for r in range(R)]),
              ((3, 0), head_steps(3, 1, False)), ((3, 1), head_steps(0, 0, False))]
    order = []
    tiles = [(layer, s, t) for (layer, s), _ in phases for t in range(R)]
    last_of_slot0 = tiles.index((3, 0, R - 1))
    for g in range(len(tiles) + OUT_LAG):
        phase, t = divmod(g, R)
        light = phases[phase][1] if phase < len(phases) else []
        first = OUT_LAG if phase else 0
        if phase == 5:
            first += 1
        spots = 4 * (R - first)
        place = 4 * (t - first)

        def light_at(q):
            at = place + q
            if at < 0:
                return []
            picked = light[-(-at * len(light) // spots):-(-(at + 1) * len(light) // spots)]
            return [st[:3] if st[0] == "code" else ("light",) + st for st in picked]

        if g < len(tiles):
            order += [("front0",) + tiles[g] + (g,)] + light_at(0)
            order += [("front1",) + tiles[g] + (g,), ("bias",) + tiles[g] + (g,)] + light_at(1)
        if 0 <= g - TURN_LAG < len(tiles):
            order += [("turn", g - TURN_LAG)]
        if g < len(tiles):
            order += light_at(2) + [("exp", g)]
        if g >= OUT_LAG:
            order += [("out",) + tiles[g - OUT_LAG] + (g - OUT_LAG,)]
        if g - OUT_LAG == last_of_slot0:
            order += [("store", 0), ("fetch", 0)]
        if g < len(tiles):
            order += light_at(3)
    return order + [("store", 1), ("fetch", 1)]


def of_next_turn(ev):
    return ev[0] == "fetch" or ev[:2] == ("code", 0) or (ev[0] == "light" and ev[2:4] == (0, 0))


USES_ACT = ("turn_h", "dst", "src", "val", "proj", "wh", "s_j")
USES_BANK = USES_ACT + ("pool",)


class Count:

    def __init__(self, sem, per, start=0):
        self.sem, self.per, self.start = sem, per, start

    def at(self, turn, done):
        return turn * self.per + self.start + done


def four_graph_layers_kernel(nc, x, adj, a0, qw, qb, kw, kb, vw, vb, pw, pb, W1, B1, W2, a2, A3, out):
    ctx = ExitStack()
    with ctx:
        def sb(name, shape, dt):
            return ctx.enter_context(nc.sbuf_tensor(name, shape, dt))

        def sem(name):
            return ctx.enter_context(nc.semaphore(name))

        code = sb("code", [P, 2, R, N], F16)
        minus = sb("minus", [P, 2, R, N], BF16)
        stage = sb("stage", [P, STAGE, N], I32)
        xs = sb("xs", [P, 2, R, D], F32)
        hn = sb("hn", [P, R, D], F32)
        hT_hi = sb("hT_hi", [P, 2, N], F16)
        hT_lo = sb("hT_lo", [P, 2, N], F16)
        src_hi = sb("src_hi", [P, TYPES, N], F16)
        src_lo = sb("src_lo", [P, TYPES, N], F16)
        dst_hi = sb("dst_hi", [P, 2, N], F16)
        dst_lo = sb("dst_lo", [P, 2, N], F16)
        val_hi = sb("val_hi", [P, 2, R, D], F16)
        val_lo = sb("val_lo", [P, 2, R, D], F16)
        z = sb("z", [P, 2, N], F32)
        probs = sb("probs", [P, 2, N], F32)
        pT_hi = sb("pT_hi", [P, 2, R, P], F16)
        pT_lo = sb("pT_lo", [P, 2, R, P], F16)
        s_j = sb("s_j", [P, 2, N], F32)
        s_i4 = sb("s_i4", [P, 2, R], F32)
        hw_hi = sb("hw_hi", [P, R, D + 1], F16)
        hw_lo = sb("hw_lo", [P, R, D], F16)
        hb = sb("hb", [P, R, D], F32)
        upd = sb("upd", [P, R, D], F32)
        type_mask = sb("type_mask", [P, N], I16)
        stats = sb("stats", [P, R, 6], F32)
        mean_var = sb("mean_var", [P, R, 2], F32)
        var_eps = sb("var_eps", [P, R], F32)
        rstd = sb("rstd", [P, R], F32)
        minus_half = sb("minus_half", [P, R], F32)
        row_max = sb("row_max", [P, 2, R], F32)
        top = sb("top", [P, 2], F32)
        exp_bias = sb("exp_bias", [P, 2], F32)
        row_sum = sb("row_sum", [P, 4], F32)
        row_inv = sb("row_inv", [P, 4], F32)
        degree = sb("degree", [P, 2], F32)
        degree_inv = sb("degree_inv", [P, 2], F32)
        m_hi = sb("m_hi", [P, TYPES, D], F16)
        m_lo = sb("m_lo", [P, TYPES, D], F16)
        m_bias = sb("m_bias", [P, TYPES], F32)
        kT_hi = sb("kT_hi", [P, D], F16)
        kT_lo = sb("kT_lo", [P, D], F16)
        v_hi = sb("v_hi", [P, D], F16)
        v_lo = sb("v_lo", [P, D], F16)
        wb_hi = sb("wb_hi", [P, 2 * D], F16)
        wb_lo = sb("wb_lo", [P, 2 * D], F16)
        w2_hi = sb("w2_hi", [P, D + 1], F16)
        w2_lo = sb("w2_lo", [P, D + 1], F16)
        wj_hi = sb("wj_hi", [P, P], F16)
        wj_lo = sb("wj_lo", [P, P], F16)
        v_bias = sb("v_bias", [P, D], F32)
        cols = sb("cols", [P, 5 + KINDS], F32)
        ident = sb("ident", [P, P], F32)
        ident_bf = sb("ident_bf", [P, P], BF16)
        ones = sb("ones", [P, P], F32)
        QB, KB, VB, AS, A3C = 0, 1, 2, 3, 5
        seen = sb("seen", [P, 1], F32)
        seen_now = sb("seen_now", [P, 1], F32)
        redo = sb("redo", [1, 1], I32)

        scores = ctx.enter_context(nc.psum_tensor("scores", [P, 4, HALF], F32))
        turned = ctx.enter_context(nc.psum_tensor("turned", [P, 2, HALF], F32))
        out_ps = ctx.enter_context(nc.psum_tensor("out_ps", [P, HALF], F32))
        head = ctx.enter_context(nc.psum_tensor("head", [P, HALF], F32))

        adj_rows = adj.rearrange("b (r p) n -> b r p n", p=P)
        x_rows = x.rearrange("b (r p) d -> b p r d", p=P)
        out_rows = out.rearrange("b (r p) d -> b p r d", p=P)

        a_raw = z[:, 0, :]
        square = probs[:, :, :].rearrange("p a (m n) -> p (a m) n", n=D)
        QW, KW, VW, PW, W1R, B1R, W2R, PBR = range(8)
        square2 = z[:, 1, :].rearrange("p (m n) -> p m n", n=D)
        PWT, W2T, VBB, WJ = range(4)

        weights_in = sem("weights_in")
        ident_step = sem("ident_step")
        const_set = sem("const_set")
        fold_ready = sem("fold_ready")
        turn_w_ready = sem("turn_w_ready")
        turn_w_out = sem("turn_w_out")
        fold2_ready = sem("fold2_ready")
        wstep = sem("wstep")
        weights_done = sem("weights_done")
        with nc.Block() as block:
            @block.sync
            def _(sp):
                sp.dma_start(a_raw, a0.rearrange("d e t -> d (e t)")).then_inc(weights_in, 16)
                for k, w in ((QW, qw), (KW, kw), (VW, vw), (PW, pw), (W1R, W1), (B1R, B1), (W2R, W2)):
                    sp.dma_start(square[:, k, :], w).then_inc(weights_in, 16)
                sp.dma_start(square[:, PBR, :], pb.rearrange("(a d) -> a d", a=1).to_broadcast([P, D])
                             ).then_inc(weights_in, 16)
                for k, v in ((QB, qb), (KB, kb), (VB, vb)):
                    sp.dma_start(cols[:, k:k + 1], v.rearrange("(d a) -> d a", a=1)).then_inc(weights_in, 16)
                with nc.allow_non_contiguous_dma(reason="a few small columns"):
                    sp.dma_start(cols[:, AS:AS + 2], a2.rearrange("(a d) -> d a", a=2)).then_inc(weights_in, 16)
                    sp.dma_start(cols[:, A3C:A3C + KINDS], A3.rearrange("k d -> d k")).then_inc(weights_in, 16)

            LOADS = 14 * 16

            @block.gpsimd
            def _(pool):
                nc.gpsimd.memset(ident[:, :], 0.0).then_inc(ident_step, 1)
                pool.wait_ge(ident_step, 1)
                nc.gpsimd.affine_select(out=ident[:, :], in_=ident[:, :], compare_op=ALU.not_equal, fill=1.0,
                                        base=0, pattern=[[-1, P]], channel_multiplier=1).then_inc(ident_step, 1)
                pool.wait_ge(ident_step, 2)
                nc.gpsimd.tensor_copy(ident_bf[:, :], ident[:, :]).then_inc(const_set, 1)
                nc.gpsimd.memset(minus_half[:, :], -0.5).then_inc(const_set, 1)
                nc.gpsimd.memset(ones[:, :], 1.0).then_inc(const_set, 1)
                nc.gpsimd.memset(hw_hi[:, :, D:D + 1], 1.0).then_inc(const_set, 1)

            @block.tensor
            def _(pe):
                pe.wait_ge(weights_in, LOADS)
                for c in range(2):
                    nc.tensor.matmul(scores[:, c, :], square[:, QW, :], a_raw[:, c * HALF:(c + 1) * HALF],
                                     start=True, stop=True)
                for t in range(TYPES):
                    mm = nc.tensor.matmul(scores[:, 2, t:t + 1], a_raw.rearrange("p (e t) -> p t e", t=TYPES)[:, t, :],
                                          cols[:, QB:QB + 1], start=True, stop=True)
                mm.then_inc(fold_ready, 1)
                pe.wait_ge(ident_step, 2)
                for k, w in enumerate((KW, PW, W2R)):
                    mm = nc.tensor.transpose(scores[:, 3, k * D:(k + 1) * D], square[:, w, :], ident[:, :])
                mm.then_inc(turn_w_ready, 1)
                pe.wait_ge(turn_w_out, 1)
                nc.tensor.matmul(turned[:, 0, 0:D], square[:, VW, :], square2[:, PWT, :], start=True, stop=True)
                nc.tensor.matmul(turned[:, 1, 0:D], square2[:, VBB, :], square2[:, PWT, :], start=True, stop=True)
                nc.tensor.matmul(out_ps[:, 0:2], square2[:, W2T, :], cols[:, AS:AS + 2],
                                 start=True, stop=True).then_inc(fold2_ready, 1)

            @block.vector
            def _(dve):
                step = [0]

                def own(ins):
                    step[0] += 1
                    ins.then_inc(wstep, 1)
                    dve.wait_ge(wstep, step[0])

                def split(hi, lo, src):
                    own(nc.vector.tensor_copy(hi, src))
                    own(nc.vector.tensor_tensor(lo, src, hi, ALU.subtract))

                own(nc.vector.memset(seen[:, :], 0.0))
                dve.wait_ge(weights_in, LOADS)
                split(wb_hi[:, 0:D], wb_lo[:, 0:D], square[:, W1R, :])
                split(wb_hi[:, D:2 * D], wb_lo[:, D:2 * D], square[:, B1R, :])
                split(w2_hi[:, 0:D], w2_lo[:, 0:D], square[:, W2R, :])
                own(nc.vector.tensor_copy(square2[:, VBB, :], cols[:, VB:VB + 1].to_broadcast([P, D])))
                dve.wait_ge(fold_ready, 1)
                for c in range(2):
                    half = scores[:, c, :].rearrange("p (e t) -> p t e", t=TYPES)
                    split(m_hi[:, :, c * 64:(c + 1) * 64], m_lo[:, :, c * 64:(c + 1) * 64], half)
                own(nc.vector.tensor_copy(m_bias[:, :], scores[:, 2, 0:TYPES]))
                dve.wait_ge(turn_w_ready, 1)
                own(nc.vector.tensor_copy(square2[:, PWT, :], scores[:, 3, D:2 * D]))
                nc.vector.tensor_copy(square2[:, W2T, :], scores[:, 3, 2 * D:3 * D]).then_inc(turn_w_out, 1)
                split(kT_hi[:, :], kT_lo[:, :], scores[:, 3, 0:D])
                dve.wait_ge(fold2_ready, 1)
                split(v_hi[:, :], v_lo[:, :], turned[:, 0, 0:D])
                own(nc.vector.tensor_tensor(v_bias[:, :], turned[:, 1, 0:D], square[:, PBR, :], ALU.add))
                split(w2_hi[:, D:D + 1], w2_lo[:, D:D + 1], out_ps[:, 0:1])
                own(nc.vector.tensor_copy(square2[:, WJ, :], out_ps[:, 1:2].to_broadcast([P, D])))
                split(wj_hi[:, :], wj_lo[:, :], square2[:, WJ, :])

        def one_pass(block, all_types, when):
            tag = "all_" if all_types else ""
            slots = 1 if all_types else 2
            types = TYPES if all_types else 2
            kinds = KINDS if all_types else 1
            turns = B // slots
            order = schedule(all_types)
            ahead = [] if all_types else sorted((ev for ev in order if of_next_turn(ev)),
                                                key=lambda ev: ("fetch", "light", "code").index(ev[0]))
            order_of_last = [ev for ev in order if ev not in ahead]

            def over_turns(engine, run):
                with when(engine):
                    if ahead:
                        run(ahead, -1)
                    with engine.Fori(0, turns - 1 if ahead else turns) as turn:
                        run(order, turn)
                    if ahead:
                        run(order_of_last, turns - 1)

            tiles = slots * 3 * R
            halves0 = slots * R * 2
            picks0 = halves0 * (types - 1)
            tiles3 = slots * R * kinds
            bank_steps = [ev[1:] for ev in order if ev[0] == "light" and ev[1] in USES_BANK]
            hi_steps = [st for st in bank_steps if st[0] in USES_ACT and st[0] != "s_j"]
            norms = [ev[1:] for ev in order if ev[0] == "light" and ev[1] == "stats"]
            banks_ahead = len([ev for ev in ahead if ev[0] == "light" and ev[1:] in bank_steps])
            his_ahead = len([ev for ev in ahead if ev[0] == "light" and ev[1:] in hi_steps])
            norms_ahead = len([ev for ev in ahead if ev[0] == "light" and ev[1:] in norms])
            tile_of = [ev[1:4] for ev in order if ev[0] == "bias"]

            def counted(name, per, start=0):
                return Count(sem(tag + name), per, start)

            x_in = [counted(f"x_in{s}", 16) for s in range(slots)]
            x_out = [counted(f"x_out{s}", 16) for s in range(slots)]
            stage_in = [counted(f"stage_in{q}", 16 * slots * R // STAGE) for q in range(STAGE)]
            code_done = counted("code_done", slots * R, start=1)
            code_used = [counted(f"code_used{s}", 1, start=1) for s in range(slots)]
            stats_done = counted("stats_done", len(norms), norms_ahead)
            rstd_done = counted("rstd_done", len(norms), norms_ahead)
            norm_done = counted("norm_done", len(norms), norms_ahead)
            head_ready = counted("head_ready", len(bank_steps), banks_ahead)
            head_hi = counted("head_hi", len(hi_steps), his_ahead)
            head_free = counted("head_free", len(bank_steps), banks_ahead)
            x_pooled = counted("x_pooled", slots)
            picks_ready = counted("picks_ready", picks0)
            picked = counted("picked", picks0)
            relu0 = counted("relu0", halves0)
            leaky0 = counted("leaky0", halves0)
            sums_ready = counted("sums_ready", slots * R)
            relu2 = counted("relu2", slots * R)
            dots_ready = counted("dots_ready", tiles3)
            relu3 = counted("relu3", slots * R)
            dots_used = counted("dots_used", tiles3)
            bias_ready = counted("bias_ready", tiles)
            probs_ready = counted("probs_ready", tiles)
            turned_ready = counted("turned_ready", 2 * tiles)
            hi_ready = counted("hi_ready", 2 * tiles)
            lo_ready = counted("lo_ready", 2 * tiles)
            inv_ready = counted("inv_ready", tiles)
            out_ready = counted("out_ready", tiles)
            x_added = counted("x_added", tiles)
            unread = sem(tag + "unread")
            own_step = sem(tag + "dve_step")
            pool_step = counted("pool_step", len(norms), norms_ahead)

            def own_steps(ev):
                if ev[0] == "light":
                    return {"stats": 1 + 2 * (ev[2] == 3 and not all_types), "norm": int(ev[2] in (0, 3)), "pool": 2,
                            "update": 1, "mask": 1 if all_types else 8,
                            "proj": int(all_types and ev[4] == 0)}.get(ev[1], 0)
                if ev[0] in ("front0", "front1") and ev[1] == 0:
                    return 6 + types - 1 if all_types else 0
                if ev[0] == "bias":
                    return {0: 0, 2: 1, 3: kinds + 3 if all_types else 0}[ev[1]]
                return 0

            own_per_turn = sum(own_steps(ev) for ev in order)
            own_ahead = sum(own_steps(ev) for ev in ahead)

            def last_tile(layer, s):
                return max(g for g, tile in enumerate(tile_of) if tile[:2] == (layer, s))

            def bank_index(st):
                return bank_steps.index(st)

            def last_bank_step(layer, s):
                k = max(k for k, st in enumerate(bank_steps) if st[1] == layer and st[2] == s)
                return k - len(bank_steps) if ("light",) + bank_steps[k] in ahead else k

            def src_row(s, t):
                return t if all_types else 2 * s + t

            def wait_apart(engine, sem, value):
                engine.wait_ge(sem, value)
                engine.sem_inc(unread, 1)

            def three(psum, lhs, rhs, start, stop):
                nc.tensor.matmul(psum, lhs[0], rhs[0], start=start, stop=False)
                nc.tensor.matmul(psum, lhs[0], rhs[1], start=False, stop=False)
                return nc.tensor.matmul(psum, lhs[1], rhs[0], start=False, stop=stop)


            @block.sync
            def _(sp):
                with when(sp), sp.Fori(0, turns) as turn:
                    for s in range(slots):
                        for r in range(R):
                            c = s * R + r
                            sp.wait_ge(code_done.sem, code_done.at(turn, s * R if r < STAGE else c - STAGE + 1))
                            sp.dma_start(stage[:, r % STAGE, :], adj_rows[turn * slots + s, r]
                                         ).then_inc(stage_in[r % STAGE].sem, 16)

            @block.gpsimd
            def _(pool):
                for count in (*code_used, code_done):
                    pool.sem_inc(count.sem, count.start)

                def run(events, turn):
                    for ev in events:
                        if ev[0] == "fetch":
                            s = ev[1]
                            later = 0 if all_types else 1
                            if later and events is not ahead:
                                pool.wait_ge(x_out[s].sem, x_out[s].at(turn, 16))
                            pool.dma_start(xs[:, s], x_rows[(turn + later) * slots + s]).then_inc(x_in[s].sem, 16)
                        elif ev[0] == "code":
                            _, s, r = ev
                            later = int(ev in ahead)
                            if r == 0 and not all_types:
                                pool.wait_ge(code_used[s].sem, code_used[s].at(turn, later))
                            ring = stage_in[r % STAGE]
                            wait_apart(pool, ring.sem, ring.at(turn, 16 * ((s + slots * later) * R // STAGE
                                                                           + r // STAGE + 1)))
                            nc.gpsimd.tensor_copy(code[:, s, r, :], stage[:, r % STAGE, :]
                                                  ).then_inc(code_done.sem, 1)
                        elif ev[0] == "light" and ev[1] == "rstd":
                            k = norms.index(("stats",) + ev[2:])
                            wait_apart(pool, stats_done.sem, stats_done.at(turn, k + 1))
                            nc.gpsimd.tensor_scalar(var_eps[:, :], mean_var[:, :, 1], EPS, None, ALU.add
                                                    ).then_inc(pool_step.sem, 1)
                            pool.wait_ge(pool_step.sem, pool_step.at(turn, k + 1))
                            nc.gpsimd.tensor_tensor(rstd[:, :], var_eps[:, :], minus_half[:, :], ALU.pow
                                                    ).then_inc(rstd_done.sem, 1)
                        elif ev[0] == "store":
                            s = ev[1]
                            wait_apart(pool, x_added.sem, x_added.at(turn, last_tile(3, s) + 1))
                            pool.dma_start(out_rows[turn * slots + s], xs[:, s]).then_inc(x_out[s].sem, 16)
                            if all_types:
                                pool.wait_ge(x_out[s].sem, x_out[s].at(turn, 16))

                over_turns(pool, run)
                if not all_types:
                    for s in range(slots):
                        pool.wait_ge(x_out[s].sem, x_out[s].at(turns - 1, 16))

            @block.tensor
            def _(pe):
                def run(events, turn):
                    for ev in events:
                        if ev[0] == "light" and ev[1] in USES_BANK:
                            _, kind, layer, s, c = ev
                            k = bank_index(ev[1:])
                            first_of_all = k == ((len(bank_steps) - banks_ahead) if events is ahead else 0)
                            if not first_of_all or (ahead and events is not ahead):
                                pe.wait_ge(head_free.sem, head_free.at(turn, k))
                            hT = (hT_hi[:, s, :], hT_lo[:, s, :])
                            if kind == "turn_h":
                                if c == 0:
                                    n = norms.index(("stats", layer, s, 0))
                                    pe.wait_ge(norm_done.sem, norm_done.at(turn, n + 1))
                                for j in range(4):
                                    mm = nc.tensor.transpose(head[:, j * P:(j + 1) * P], hn[:, 4 * c + j, :],
                                                             ident[:, :])
                            elif kind in ("dst", "src", "s_j"):
                                t, c = divmod(c, 2)
                                w = {"dst": (kT_hi[:, :], kT_lo[:, :]), "src": (m_hi[:, t, :], m_lo[:, t, :]),
                                     "s_j": (wj_hi[:, :], wj_lo[:, :])}[kind]
                                ks = slice(c * HALF, (c + 1) * HALF)
                                mm = three(head[:, :], w, (hT[0][:, ks], hT[1][:, ks]), True, True)
                            elif kind in ("val", "proj", "wh"):
                                w, width, per = {"val": ((v_hi, v_lo), D, 4), "proj": ((wb_hi, wb_lo), 2 * D, 2),
                                                 "wh": ((w2_hi, w2_lo), D + 1, 3)}[kind]
                                for j in range(min(per, R - c * per)):
                                    ns = slice((c * per + j) * P, (c * per + j + 1) * P)
                                    mm = three(head[:, j * width:(j + 1) * width],
                                               (hT[0][:, ns], hT[1][:, ns]), (w[0][:, :], w[1][:, :]), True, True)
                            elif kind == "pool":
                                if c == 0 and not all_types:
                                    pe.wait_ge(code_done.sem, code_done.at(turn, (s + 1) * R))
                                edges = minus if all_types else code
                                for j in range(2):
                                    ns = slice((2 * c + j) * P, (2 * c + j + 1) * P)
                                    o = j * (D + 1)
                                    for r in range(R):
                                        e = (edges[:, s, r, ns].bitcast(F16) if all_types else edges[:, s, r, ns])
                                        hi = (head[:, o:o + D + 1], e, hw_hi[:, r, :])
                                        lo = (head[:, o:o + D], e, hw_lo[:, r, :])
                                        if r == 0:
                                            nc.tensor.matmul(*hi, start=True, stop=False)
                                            nc.tensor.matmul(*lo, start=False, stop=False)
                                        else:
                                            nc.tensor.matmul(*lo, start=False, stop=False)
                                            mm = nc.tensor.matmul(*hi, start=False, stop=(r == R - 1))
                            mm.then_inc(head_ready.sem, 1)

                        elif ev[0] in ("front0", "front1") and ev[1] == 0:
                            _, _, s, t, g = ev
                            hf = int(ev[0] == "front1")
                            h = 2 * (s * R + t) + hf
                            ks = slice(hf * HALF, (hf + 1) * HALF)
                            qs = slice(t * P, (t + 1) * P)
                            if t == 0 and hf == 0:
                                pe.wait_ge(head_free.sem, head_free.at(turn, last_bank_step(0, s) + 1))
                            for ty in range(types):
                                v = h * (types - 1) + ty - 1
                                if ty == 0 and h >= 2:
                                    pe.wait_ge(leaky0.sem, leaky0.at(turn, h - 1))
                                if ty >= 2:
                                    pe.wait_ge(picked.sem, picked.at(turn, v))
                                row = src_row(s, ty)
                                mm = three(scores[:, 2 * hf + min(ty, 1), :],
                                           (src_hi[:, row, qs], src_lo[:, row, qs]),
                                           (dst_hi[:, s, ks], dst_lo[:, s, ks]), True, True)
                                if ty:
                                    mm.then_inc(picks_ready.sem, 1)

                        elif ev[0] == "front0" and ev[1] == 3:
                            _, _, s, t, g = ev
                            if t == 0:
                                pe.wait_ge(head_free.sem, head_free.at(turn, last_bank_step(3, s) + 1))
                            qs = slice(t * P, (t + 1) * P)
                            for kd in range(kinds):
                                w = (s * R + t) * kinds + kd
                                if w >= 2:
                                    pe.wait_ge(dots_used.sem, dots_used.at(turn, w - 1))
                                row = src_row(s, kd)
                                for hf in range(2):
                                    ks = slice(hf * HALF, (hf + 1) * HALF)
                                    bank = scores[:, 2 * (w % 2) + hf, :]
                                    mm = three(bank, (src_hi[:, row, qs], src_lo[:, row, qs]),
                                               (hT_hi[:, s, ks], hT_lo[:, s, ks]), True, all_types)
                                    if not all_types:
                                        mm = nc.tensor.matmul(bank, ident_bf[:, :], minus[:, s, t, ks],
                                                              start=False, stop=True)
                                mm.then_inc(dots_ready.sem, 1)

                        elif ev[0] == "turn":
                            g = ev[1]
                            pe.wait_ge(probs_ready.sem, probs_ready.at(turn, g + 1))
                            for hf in range(2):
                                if g >= 1:
                                    pe.wait_ge(lo_ready.sem, lo_ready.at(turn, 2 * g + hf - 1))
                                for j in range(4):
                                    c = 4 * hf + j
                                    mm = nc.tensor.transpose(turned[:, hf, j * P:(j + 1) * P],
                                                             probs[:, g % 2, c * P:(c + 1) * P], ident[:, :])
                                mm.then_inc(turned_ready.sem, 1)

                        elif ev[0] == "out":
                            _, layer, s, t, g = ev
                            pe.wait_ge(lo_ready.sem, lo_ready.at(turn, 2 * g + 2))
                            if g >= 1:
                                pe.wait_ge(x_added.sem, x_added.at(turn, g))
                            for c in range(R):
                                mm = three(out_ps[:, 0:D], (pT_hi[:, g % 2, c, :], pT_lo[:, g % 2, c, :]),
                                           (val_hi[:, s, c, :], val_lo[:, s, c, :]), c == 0, c == R - 1)
                            mm.then_inc(out_ready.sem, 1)

                over_turns(pe, run)

            @block.scalar
            def _(act):
                def run(events, turn):
                    for ev in events:
                        if ev[0] == "light" and ev[1] in USES_ACT:
                            _, kind, layer, s, c = ev
                            k = bank_index(ev[1:])
                            act.wait_ge(head_ready.sem, head_ready.at(turn, k + 1))
                            if kind == "turn_h":
                                ks = slice(c * HALF, (c + 1) * HALF)
                                ins = nc.scalar.activation(hT_hi[:, s, ks], head[:, :], ACT.Relu)
                                if layer == 3:
                                    for kd in range(kinds):
                                        nc.scalar.activation(src_hi[:, src_row(s, kd), ks], head[:, :], ACT.Identity,
                                                             scale=cols[:, A3C + kd:A3C + kd + 1])
                                    ins = nc.scalar.activation(
                                        val_hi[:, s, 4 * c:4 * c + 4, :], hn[:, 4 * c:4 * c + 4, :], ACT.Copy)
                            elif kind in ("dst", "src"):
                                t, c = divmod(c, 2)
                                ks = slice(c * HALF, (c + 1) * HALF)
                                if kind == "dst":
                                    ins = nc.scalar.activation(dst_hi[:, s, ks], head[:, :], ACT.Identity,
                                                               bias=cols[:, KB:KB + 1])
                                else:
                                    ins = nc.scalar.activation(src_hi[:, src_row(s, t), ks], head[:, :],
                                                               ACT.Identity, bias=m_bias[:, t:t + 1])
                            elif kind == "val":
                                ins = nc.scalar.activation(val_hi[:, s, 4 * c:4 * c + 4, :],
                                                           head[:, :].rearrange("p (j d) -> p j d", d=D), ACT.Copy)
                            elif kind == "proj":
                                two = head[:, :].rearrange("p (j d) -> p j d", d=2 * D)
                                nc.scalar.activation(hw_hi[:, 2 * c:2 * c + 2, 0:D], two[:, :, 0:D], ACT.Copy)
                                ins = nc.scalar.activation(hb[:, 2 * c:2 * c + 2, :], two[:, :, D:2 * D], ACT.Copy)
                            elif kind == "wh":
                                n = min(3, R - 3 * c)
                                rows = head[:, 0:n * (D + 1)].rearrange("p (j d) -> p j d", d=D + 1)
                                ins = nc.scalar.activation(val_hi[:, s, 3 * c:3 * c + n, :], rows[:, :, 0:D], ACT.Copy)
                            elif kind == "s_j":
                                nc.scalar.activation(s_j[:, s, c * HALF:(c + 1) * HALF], head[:, :],
                                                     ACT.Copy).then_inc(head_free.sem, 1)
                                continue
                            ins.then_inc(head_hi.sem, 1)

                        elif ev[0] in ("front0", "front1") and ev[1] == 0:
                            _, _, s, t, g = ev
                            hf = int(ev[0] == "front1")
                            h = 2 * (s * R + t) + hf
                            act.wait_ge(picked.sem, picked.at(turn, (h + 1) * (types - 1)))
                            if hf == 0 and g >= 2:
                                act.wait_ge(turned_ready.sem, turned_ready.at(turn, 2 * g - 2))
                            nc.scalar.activation(probs[:, g % 2, hf * HALF:(hf + 1) * HALF], scores[:, 2 * hf, :],
                                                 ACT.Relu, scale=4.0).then_inc(relu0.sem, 1)

                        elif ev[0] == "front1" and ev[1] == 2:
                            _, _, s, t, g = ev
                            act.wait_ge(sums_ready.sem, sums_ready.at(turn, s * R + t + 1))
                            if g >= 2:
                                act.wait_ge(turned_ready.sem, turned_ready.at(turn, 2 * g - 2))
                            nc.scalar.activation(probs[:, g % 2, :], z[:, g % 2, :], ACT.Relu,
                                                 bias=s_i4[:, s, t:t + 1], scale=4.0).then_inc(relu2.sem, 1)

                        elif ev[0] == "front1" and ev[1] == 3 and not all_types:
                            _, _, s, t, g = ev
                            u = s * R + t
                            act.wait_ge(dots_ready.sem, dots_ready.at(turn, u + 1))
                            act.wait_ge(turned_ready.sem, turned_ready.at(turn, 2 * g - 2))
                            pair = scores[:, 2 * (u % 2):2 * (u % 2) + 2, :].rearrange("p a n -> p (a n)")
                            nc.scalar.activation(probs[:, g % 2, :], pair, ACT.Relu, scale=4.0
                                                 ).then_inc(relu3.sem, 1)

                        elif ev[0] == "exp":
                            g = ev[1]
                            act.wait_ge(bias_ready.sem, bias_ready.at(turn, g + 1))
                            if tile_of[g][0] == 3 and all_types:
                                act.wait_ge(turned_ready.sem, turned_ready.at(turn, 2 * g - 2))
                            nc.scalar.activation(probs[:, g % 2, :], z[:, g % 2, :], ACT.Exp,
                                                 bias=exp_bias[:, g % 2:g % 2 + 1],
                                                 accum_out=row_sum[:, g % 4:g % 4 + 1]).then_inc(probs_ready.sem, 1)

                        elif ev[0] == "turn":
                            g = ev[1]
                            if g >= 2:
                                act.wait_ge(out_ready.sem, out_ready.at(turn, g - 1))
                            for hf in range(2):
                                act.wait_ge(turned_ready.sem, turned_ready.at(turn, 2 * g + hf + 1))
                                nc.scalar.activation(pT_hi[:, g % 2, 4 * hf:4 * hf + 4, :],
                                                     turned[:, hf, :].rearrange("p (j i) -> p j i", i=P),
                                                     ACT.Copy).then_inc(hi_ready.sem, 1)

                over_turns(act, run)

            @block.vector
            def _(dve):
                own = [0]

                def run(events, turn):
                    own[0] = own_per_turn - own_ahead if events is ahead else 0

                    def settled(ins, apart=False):
                        own[0] += 1
                        ins.then_inc(own_step, 1)
                        value = turn * own_per_turn + own_ahead + own[0]
                        if apart:
                            wait_apart(dve, own_step, value)
                        else:
                            dve.wait_ge(own_step, value)

                    def pick_type(value, ks, s, t):
                        settled(nc.vector.tensor_scalar(type_mask[:, ks], code[:, s, t, ks], value, None,
                                                        ALU.is_equal), apart=True)

                    def leaky_half(turn, s, t, g, hf):
                        h = 2 * (s * R + t) + hf
                        ks = slice(hf * HALF, (hf + 1) * HALF)
                        mx = top[:, g % 2:g % 2 + 1]
                        if hf == 0 and g >= 2:
                            dve.wait_ge(probs_ready.sem, probs_ready.at(turn, g - 1))
                        if hf == 1:
                            dve.wait_ge(leaky0.sem, leaky0.at(turn, h))
                        wait_apart(dve, relu0.sem, relu0.at(turn, h + 1))
                        nc.vector.tensor_tensor_reduce(z[:, g % 2, ks], scores[:, 2 * hf, :], probs[:, g % 2, ks], 0.2,
                                                       mx if hf else LOWEST, ALU.add, ALU.max, mx
                                                       ).then_inc(leaky0.sem, 1)

                    for ev in events:
                        if ev[0] == "light":
                            _, kind, layer, s, c = ev
                            n = norms.index(("stats", layer, s, 0))
                            if kind in USES_BANK:
                                k = bank_index(ev[1:])
                            if ev[1:] in hi_steps:
                                dve.wait_ge(head_hi.sem, head_hi.at(turn, hi_steps.index(ev[1:]) + 1))

                            if kind == "stats":
                                if layer == 0:
                                    dve.wait_ge(x_in[s].sem, x_in[s].at(turn, 32 if ev in ahead else 16))
                                elif layer == 2:
                                    dve.wait_ge(x_pooled.sem, x_pooled.at(turn, s + 1))
                                else:
                                    dve.wait_ge(x_added.sem, x_added.at(turn, last_tile(layer - 1, s) + 1))
                                if layer == 3 and not all_types:
                                    settled(nc.vector.tensor_reduce(seen_now[:, :], row_max[:, s, :], AX.X,
                                                                    ALU.min))
                                    settled(nc.vector.scalar_tensor_tensor(seen[:, :], seen_now[:, :], 0.5 * MASKED,
                                                                           seen[:, :], ALU.is_lt, ALU.max))
                                for r in range(R):
                                    ins = nc.vector.bn_stats(stats[:, r, :], xs[:, s, r, :])
                                settled(ins, apart=True)
                                for r in range(R):
                                    ins = nc.vector.bn_aggr(mean_var[:, r, :], stats[:, r, :])
                                ins.then_inc(stats_done.sem, 1)
                            elif kind == "norm":
                                dve.wait_ge(rstd_done.sem, rstd_done.at(turn, n + 1))
                                for r in range(R):
                                    ins = nc.vector.tensor_scalar(hn[:, r, :], xs[:, s, r, :], mean_var[:, r, 0:1],
                                                                  rstd[:, r:r + 1], ALU.subtract, ALU.mult)
                                if layer == 3:
                                    settled(ins)
                                    ins = nc.vector.tensor_scalar(hn[:, :, :], hn[:, :, :], 0.0, None, ALU.max)
                                ins.then_inc(norm_done.sem, 1)
                                if layer == 0:
                                    dve.wait_ge(norm_done.sem, norm_done.at(turn, n + 1))
                                    settled(nc.vector.tensor_tensor(
                                        xs[:, s], xs[:, s], v_bias[:, None, :].to_broadcast([P, R, D]), ALU.add))
                            elif kind == "turn_h":
                                ks = slice(c * HALF, (c + 1) * HALF)
                                ins = nc.vector.scalar_tensor_tensor(hT_lo[:, s, ks], head[:, :], 0.0,
                                                                     hT_hi[:, s, ks], ALU.max, ALU.subtract)
                                if layer == 3:
                                    for kd in range(kinds):
                                        row = src_row(s, kd)
                                        nc.vector.scalar_tensor_tensor(
                                            src_lo[:, row, ks], head[:, :], cols[:, A3C + kd:A3C + kd + 1],
                                            src_hi[:, row, ks], ALU.mult, ALU.subtract)
                                    rs = slice(4 * c, 4 * c + 4)
                                    ins = nc.vector.tensor_tensor(val_lo[:, s, rs, :], hn[:, rs, :],
                                                                  val_hi[:, s, rs, :], ALU.subtract)
                                ins.then_inc(head_free.sem, 1)
                            elif kind == "dst":
                                ks = slice(c * HALF, (c + 1) * HALF)
                                nc.vector.scalar_tensor_tensor(dst_lo[:, s, ks], head[:, :], cols[:, KB:KB + 1],
                                                               dst_hi[:, s, ks], ALU.add, ALU.subtract
                                                               ).then_inc(head_free.sem, 1)
                            elif kind == "src":
                                t, c = divmod(c, 2)
                                ks = slice(c * HALF, (c + 1) * HALF)
                                row = src_row(s, t)
                                nc.vector.scalar_tensor_tensor(src_lo[:, row, ks], head[:, :], m_bias[:, t:t + 1],
                                                               src_hi[:, row, ks], ALU.add, ALU.subtract
                                                               ).then_inc(head_free.sem, 1)
                            elif kind == "val":
                                rs = slice(4 * c, 4 * c + 4)
                                nc.vector.tensor_tensor(val_lo[:, s, rs, :],
                                                        head[:, :].rearrange("p (j d) -> p j d", d=D),
                                                        val_hi[:, s, rs, :], ALU.subtract
                                                        ).then_inc(head_free.sem, 1)
                            elif kind == "proj":
                                if c == 0 and all_types:
                                    dve.wait_ge(code_done.sem, code_done.at(turn, (s + 1) * R))
                                    settled(nc.vector.tensor_scalar(minus[:, s].bitcast(F16), code[:, s], 0.0, None,
                                                                    ALU.not_equal))
                                two = head[:, :].rearrange("p (j d) -> p j d", d=2 * D)
                                nc.vector.tensor_tensor(hw_lo[:, 2 * c:2 * c + 2, :], two[:, :, 0:D],
                                                        hw_hi[:, 2 * c:2 * c + 2, 0:D], ALU.subtract
                                                        ).then_inc(head_free.sem, 1)
                            elif kind == "pool":
                                two = head[:, 0:2 * (D + 1)].rearrange("p (j d) -> p j d", d=D + 1)
                                dve.wait_ge(head_ready.sem, head_ready.at(turn, k + 1))
                                settled(nc.vector.tensor_scalar(degree[:, :], two[:, :, D], 1.0, None, ALU.max))
                                settled(nc.vector.reciprocal(degree_inv[:, :], degree[:, :]))
                                for j in range(2):
                                    ins = nc.vector.scalar_tensor_tensor(
                                        upd[:, 2 * c + j, :], two[:, j, 0:D], degree_inv[:, j:j + 1],
                                        hb[:, 2 * c + j, :], ALU.mult, ALU.add)
                                ins.then_inc(head_free.sem, 1)
                            elif kind == "update":
                                dve.wait_ge(head_free.sem, head_free.at(turn, last_bank_step(1, s) + 1))
                                settled(nc.vector.scalar_tensor_tensor(upd[:, :, :], upd[:, :, :], 0.1, upd[:, :, :],
                                                                       ALU.mult, ALU.max))
                                nc.vector.tensor_tensor(xs[:, s], xs[:, s], upd[:, :, :], ALU.add
                                                        ).then_inc(x_pooled.sem, 1)
                            elif kind == "wh":
                                m = min(3, R - 3 * c)
                                rows = head[:, 0:m * (D + 1)].rearrange("p (j d) -> p j d", d=D + 1)
                                nc.vector.tensor_scalar(s_i4[:, s, 3 * c:3 * c + m], rows[:, :, D], 4.0, None, ALU.mult)
                                nc.vector.tensor_tensor(val_lo[:, s, 3 * c:3 * c + m, :], rows[:, :, 0:D],
                                                        val_hi[:, s, 3 * c:3 * c + m, :], ALU.subtract
                                                        ).then_inc(head_free.sem, 1)
                            elif kind == "mask":
                                dve.wait_ge(code_done.sem, code_done.at(turn, (s + 1) * R))
                                if not all_types:
                                    word = [code[:, s, 2 * q:2 * q + 2, :].rearrange("p r n -> p (r n)").bitcast(I32)
                                            for q in range(4)]
                                    a = hn[:, :, :].rearrange("p r d -> p (r d)").bitcast(I32)
                                    b = upd[:, :, :].rearrange("p r d -> p (r d)").bitcast(I32)
                                    settled(nc.vector.tensor_tensor(a, word[0], word[1], ALU.bitwise_or))
                                    settled(nc.vector.tensor_tensor(b, word[2], word[3], ALU.bitwise_or))
                                    settled(nc.vector.tensor_tensor(a, a, b, ALU.bitwise_or))
                                    settled(nc.vector.tensor_tensor(b[:, 0:512], a[:, 0:512], a[:, 512:1024],
                                                                    ALU.bitwise_or))
                                    settled(nc.vector.tensor_tensor(a[:, 0:256], b[:, 0:256], b[:, 256:512],
                                                                    ALU.bitwise_or))
                                    settled(nc.vector.tensor_reduce(seen_now[:, :], a[:, 0:256].bitcast(U16), AX.X,
                                                                    ALU.max))
                                    settled(nc.vector.scalar_tensor_tensor(seen[:, :], seen_now[:, :], float(BITS_OF_1),
                                                                           seen[:, :], ALU.is_gt, ALU.max))
                                settled(nc.vector.tensor_scalar(minus[:, s], code[:, s], 0.0, MASKED,
                                                                ALU.is_equal, ALU.mult))
                                nc.vector.tensor_copy(degree[:, 0:1], degree_inv[:, 0:1]
                                                      ).then_inc(code_used[s].sem, 1)

                        elif ev[0] in ("front0", "front1") and ev[1] == 0:
                            _, _, s, t, g = ev
                            hf = int(ev[0] == "front1")
                            h = 2 * (s * R + t) + hf
                            ks = slice(hf * HALF, (hf + 1) * HALF)
                            if t == 0 and hf == 0:
                                dve.wait_ge(code_done.sem, code_done.at(turn, (s + 1) * R))
                            for ty in range(1, types):
                                v = h * (types - 1) + ty - 1
                                wait_apart(dve, picks_ready.sem, picks_ready.at(turn, v + 1))
                                base = scores[:, 2 * hf, :]
                                if not all_types:
                                    mask = code[:, s, t, ks].bitcast(I16)
                                else:
                                    if ty == 1:
                                        for op, bound, fill in ((ALU.is_equal, -1.0, MASKED),
                                                                (ALU.is_gt, TYPES - 1.0, -LOWEST)):
                                            settled(nc.vector.tensor_scalar(type_mask[:, ks], code[:, s, t, ks],
                                                                            bound, None, op))
                                            settled(nc.vector.memset(s_j[:, 0, ks], fill), apart=True)
                                            settled(nc.vector.copy_predicated(base, type_mask[:, ks],
                                                                              s_j[:, 0, ks]))
                                    pick_type(float(ty), ks, s, t)
                                    mask = type_mask[:, ks]
                                nc.vector.copy_predicated(base, mask, scores[:, 2 * hf + 1, :]
                                                          ).then_inc(picked.sem, 1)
                                if all_types:
                                    dve.wait_ge(picked.sem, picked.at(turn, v + 1))
                            if hf == 1:
                                leaky_half(turn, s, t, g, 0)

                        elif ev[0] == "front0" and ev[1] == 2:
                            _, _, s, t, g = ev
                            if t == 0:
                                dve.wait_ge(head_free.sem, head_free.at(turn, last_bank_step(2, s) + 1))
                            wait_apart(dve, probs_ready.sem, probs_ready.at(turn, g - 1))
                            nc.vector.tensor_tensor_reduce(z[:, g % 2, :], s_j[:, s, :], minus[:, s, t, :], 1.0, LOWEST,
                                                           ALU.add, ALU.max, row_max[:, s, t:t + 1]
                                                           ).then_inc(sums_ready.sem, 1)

                        elif ev[0] == "bias":
                            _, layer, s, t, g = ev
                            u = s * R + t
                            zt, relu, mx = z[:, g % 2, :], probs[:, g % 2, :], top[:, g % 2:g % 2 + 1]
                            eb = exp_bias[:, g % 2:g % 2 + 1]
                            if layer == 0:
                                leaky_half(turn, s, t, g, 1)
                                dve.wait_ge(leaky0.sem, leaky0.at(turn, 2 * u + 2))
                                nc.vector.tensor_scalar(eb, mx, -1024.0, 1.0 / 1024, ALU.mult, ALU.mult
                                                        ).then_inc(bias_ready.sem, 1)
                            elif layer == 2:
                                wait_apart(dve, relu2.sem, relu2.at(turn, u + 1))
                                settled(nc.vector.tensor_tensor_reduce(zt, zt, relu, 0.2, LOWEST, ALU.add, ALU.max, mx))
                                nc.vector.tensor_scalar(eb, mx, -1024.0, 1.0 / 1024, ALU.mult, ALU.mult
                                                        ).then_inc(bias_ready.sem, 1)
                            else:
                                dve.wait_ge(probs_ready.sem, probs_ready.at(turn, g - 1))
                                if not all_types:
                                    wait_apart(dve, relu3.sem, relu3.at(turn, u + 1))
                                    pair = scores[:, 2 * (u % 2):2 * (u % 2) + 2, :].rearrange("p a n -> p (a n)")
                                    nc.vector.tensor_tensor_reduce(zt, pair, relu, 0.2, LOWEST, ALU.add, ALU.max, mx
                                                                   ).then_inc(dots_used.sem, 1)
                                    dve.wait_ge(dots_used.sem, dots_used.at(turn, u + 1))
                                    nc.vector.tensor_scalar(eb, mx, -1.0, None, ALU.mult
                                                            ).then_inc(bias_ready.sem, 1)
                                else:
                                    settled(nc.vector.memset(zt, LAYER3_NONE))
                                    for kd in range(kinds):
                                        w = u * kinds + kd
                                        dve.wait_ge(dots_ready.sem, dots_ready.at(turn, w + 1))
                                        pair = scores[:, 2 * (w % 2):2 * (w % 2) + 2, :].rearrange("p a n -> p (a n)")
                                        pick_type(kd + 1.0, slice(0, N), s, t)
                                        nc.vector.copy_predicated(zt, type_mask[:, :], pair
                                                                  ).then_inc(dots_used.sem, 1)
                                        dve.wait_ge(dots_used.sem, dots_used.at(turn, w + 1))
                                    settled(nc.vector.scalar_tensor_tensor(zt, zt, 0.2, zt, ALU.mult, ALU.max))
                                    settled(nc.vector.tensor_reduce(mx, zt, AX.X, ALU.max))
                                    nc.vector.tensor_scalar(eb, mx, -1.0, None, ALU.mult
                                                            ).then_inc(bias_ready.sem, 1)

                        elif ev[0] == "turn":
                            g = ev[1]
                            for hf in range(2):
                                dve.wait_ge(hi_ready.sem, hi_ready.at(turn, 2 * g + hf + 1))
                                nc.vector.tensor_tensor(pT_lo[:, g % 2, 4 * hf:4 * hf + 4, :],
                                                        turned[:, hf, :].rearrange("p (j i) -> p j i", i=P),
                                                        pT_hi[:, g % 2, 4 * hf:4 * hf + 4, :], ALU.subtract
                                                        ).then_inc(lo_ready.sem, 1)
                            nc.vector.reciprocal(row_inv[:, g % 4:g % 4 + 1], row_sum[:, g % 4:g % 4 + 1]
                                                 ).then_inc(inv_ready.sem, 1)

                        elif ev[0] == "out":
                            _, layer, s, t, g = ev
                            dve.wait_ge(out_ready.sem, out_ready.at(turn, g + 1))
                            dve.wait_ge(inv_ready.sem, inv_ready.at(turn, g + 1))
                            nc.vector.scalar_tensor_tensor(xs[:, s, t, :], out_ps[:, 0:D],
                                                           row_inv[:, g % 4:g % 4 + 1], xs[:, s, t, :],
                                                           ALU.mult, ALU.add).then_inc(x_added.sem, 1)
                    assert own[0] == own_per_turn - (own_ahead if events is order_of_last and ahead else 0)

                over_turns(dve, run)

        with nc.Block() as block:
            one_pass(block, False, lambda engine: nullcontext())

        witness_sum = sem("witness_sum")
        redo_ready = sem("redo_ready")
        with nc.Block() as block:
            @block.vector
            def _(dve):
                dve.wait_ge(witness_sum, 1)
                nc.vector.tensor_copy(redo[:, :], head[0:1, 0:1]).then_inc(redo_ready, 1)

            @block.tensor
            def _(pe):
                nc.tensor.matmul(head[0:1, 0:1], seen[:, 0:1], ones[:, 0:1], start=True, stop=True
                                 ).then_inc(witness_sum, 1)

        @contextmanager
        def if_seen(engine):
            engine.wait_ge(redo_ready, 1)
            with engine.If(engine.value_load(redo[0:1, 0:1]) != 0):
                yield

        with nc.Block() as block:
            one_pass(block, True, if_seen)


_INS = ["x", "adj", "L0_gnn_a", "L0_gnn_qw", "L0_gnn_qb", "L0_gnn_kw", "L0_gnn_kb", "L0_gnn_vw", "L0_gnn_vb",
        "L0_gnn_pw", "L0_gnn_pb", "L1_gnn_W", "L1_gnn_B", "L2_gnn_W", "L2_gnn_a", "L3_gnn_A"]


def kernel(**inputs):
    import numpy as _np
    import concourse.bacc as _bacc
    from concourse import mybir as _mybir
    from concourse.bass_utils import run_bass_kernel_spmd as _run

    nc = _bacc.Bacc("TRN2", target_bir_lowering=False, num_devices=1)
    arrays, args = {}, []
    for name in _INS:
        a = _np.ascontiguousarray(inputs[name])
        arrays[f"in_{name}"] = a
        args.append(nc.dram_tensor(f"in_{name}", a.shape, _mybir.dt.from_np(a.dtype), kind="ExternalInput").ap())
    args.append(nc.dram_tensor("out_x", (B, N, D), _mybir.dt.float32, kind="ExternalOutput").ap())
    four_graph_layers_kernel(nc, *args)
    r = _run(nc, [arrays], core_ids=[0])
    return r.results[0]["out_x"]
```

```python
from contextlib import ExitStack, contextmanager, nullcontext

import concourse.bass as bass
from concourse import mybir

B, N, D, P = 8, 1024, 128, 128
R = N // P
HALF = N // 2
TYPES = 8
KINDS = 4
HEADS = 3
STAGE = 4
TURN_LAG, OUT_LAG = 1, 2
EPS = 1e-5
MASKED = -1.0e37
LOWEST = -3.0e38
LAYER3_NONE = -9.0e15
BITS_OF_1 = 0x3C00

ALU = mybir.AluOpType
ACT = mybir.ActivationFunctionType
AX = mybir.AxisListType
F32, F16, BF16 = mybir.dt.float32, mybir.dt.float16, mybir.dt.bfloat16
I32, I16, U16 = mybir.dt.int32, mybir.dt.int16, mybir.dt.uint16


USES_ACT = ("turn_h", "dst", "src", "val", "proj", "wh", "s_j")
USES_BANK = USES_ACT + ("pool",)


def code_steps(s, all_types):
    return [("witness", 2, s, c) for c in range(0 if all_types else 4)] + [("mask", 2, s, c) for c in range(4)]


def middle_steps(s):
    first, then = head_steps(1, s, False), head_steps(2, s, False)
    codes = code_steps(s, False)
    long = next(k for k, st in enumerate(first) if st[0] == "proj")
    steps = first[:long]
    for k, st in enumerate(first[long:]):
        steps += [st] + codes[k:k + 1] * (k < len(codes) - 1)
    long = next(k for k, st in enumerate(then) if st[0] == "wh")
    return steps + then[:long + 1] + codes[-1:] + [st for st in then[long + 1:] if st not in codes]


def head_steps(layer, s, all_types):
    steps = [("stats", layer, s, c) for c in range(2)] + [("rstd", layer, s, 0)]
    steps += [("norm", layer, s, c) for c in range(2)]
    steps += [("turn_h", layer, s, c) for c in range(2)]
    if layer == 0:
        steps += [("dst", layer, s, c) for c in range(2)]
        steps += [("src", layer, s, 2 * t + c) for t in range(TYPES if all_types else 2) for c in range(2)]
        steps += [("val", layer, s, c) for c in range(2)]
    if layer == 1:
        steps += [("proj", layer, s, c) for c in range(4)]
        steps += [("pool", layer, s, c) for c in range(4)]
        steps += [("update", layer, s, c) for c in range(2)]
    if layer == 2:
        steps += [("wh", layer, s, c) for c in range(3)]
        steps += [("s_j", layer, s, c) for c in range(2)]
        steps += code_steps(s, all_types)
    return steps


def schedule(all_types):
    if all_types:
        order, tile = [("fetch", 0)] + [("code", 0, r) for r in range(R)], 0
        for layer in (0, 1, 2, 3):
            for st in head_steps(layer, 0, True):
                order += [("light",) + st] + [("late",) + st] * (st[0] in USES_BANK)
            if layer == 1:
                continue
            for t in range(R + OUT_LAG):
                if t < R:
                    order += [("front0", layer, 0, t, tile + t), ("front1", layer, 0, t, tile + t),
                              ("bias", layer, 0, t, tile + t)]
                if 0 <= t - TURN_LAG < R:
                    order += [("turn", tile + t - TURN_LAG)]
                if t < R:
                    order += [("exp", tile + t)]
                if 0 <= t - OUT_LAG < R:
                    order += [("out", layer, 0, t - OUT_LAG, tile + t - OUT_LAG)]
            tile += R
        return order + [("store", 0)]

    phases = [((0, 0), head_steps(0, 1, False) + [("code", 1, r, 0) for r in range(R)]),
              ((0, 1), middle_steps(0)), ((2, 0), middle_steps(1)),
              ((2, 1), head_steps(3, 0, False) + [("code", 0, r, 0) for r in range(R)]),
              ((3, 0), head_steps(3, 1, False)), ((3, 1), head_steps(0, 0, False))]
    order = []
    tiles = [(layer, s, t) for (layer, s), _ in phases for t in range(R)]
    waiting = []

    def late_parts():
        parts = waiting[:]
        waiting.clear()
        return parts

    last_of_slot0 = tiles.index((3, 0, R - 1))
    for g in range(len(tiles) + OUT_LAG):
        phase, t = divmod(g, R)
        light = phases[phase][1] if phase < len(phases) else []
        first = OUT_LAG
        if phase == 5:
            first += 1
        spots = 4 * (R - first)
        place = 4 * (t - first)

        def light_at(q):
            at = place + q
            if at < 0:
                return late_parts()
            picked = light[-(-at * len(light) // spots):-(-(at + 1) * len(light) // spots)]
            placed = late_parts()
            for st in picked:
                placed += late_parts() + [st[:3] if st[0] == "code" else ("light",) + st]
                if st[0] in USES_BANK and phases[phase][0][0] == 2:
                    waiting.append(("late",) + st)
                elif st[0] in USES_BANK:
                    placed.append(("late",) + st)
            return placed

        if t == 0:
            order += late_parts()
        if g < len(tiles):
            order += [("front0",) + tiles[g] + (g,)] + light_at(0)
            order += [("front1",) + tiles[g] + (g,), ("bias",) + tiles[g] + (g,)] + light_at(1)
        if 0 <= g - TURN_LAG < len(tiles):
            order += [("turn", g - TURN_LAG)]
        if g < len(tiles):
            order += light_at(2) + [("exp", g)]
        if g >= OUT_LAG:
            order += [("out",) + tiles[g - OUT_LAG] + (g - OUT_LAG,)]
        if g - OUT_LAG == last_of_slot0:
            order += [("store", 0), ("fetch", 0)]
        if g < len(tiles):
            order += light_at(3)
    return order + [("store", 1), ("fetch", 1)]


def of_next_turn(ev):
    return ev[0] == "fetch" or ev[:2] == ("code", 0) or (ev[0] in ("light", "late") and ev[2:4] == (0, 0))


class Count:

    def __init__(self, sem, per, start=0):
        self.sem, self.per, self.start = sem, per, start

    def at(self, turn, done):
        return turn * self.per + self.start + done


def four_graph_layers_kernel(nc, x, adj, a0, qw, qb, kw, kb, vw, vb, pw, pb, W1, B1, W2, a2, A3, out):
    ctx = ExitStack()
    with ctx:
        def sb(name, shape, dt):
            return ctx.enter_context(nc.sbuf_tensor(name, shape, dt))

        def sem(name):
            return ctx.enter_context(nc.semaphore(name))

        code = sb("code", [P, 2, R, N], F16)
        minus = sb("minus", [P, 2, R, N], BF16)
        stage = sb("stage", [P, STAGE, N], I32)
        xs = sb("xs", [P, 2, R, D], F32)
        hn = sb("hn", [P, R, D], F32)
        hT_hi = sb("hT_hi", [P, 2, N], F16)
        hT_lo = sb("hT_lo", [P, 2, N], F16)
        src_hi = sb("src_hi", [P, TYPES, N], F16)
        src_lo = sb("src_lo", [P, TYPES, N], F16)
        dst_hi = sb("dst_hi", [P, 2, N], F16)
        dst_lo = sb("dst_lo", [P, 2, N], F16)
        val = sb("val", [P, 2, 2, R, D], F16)
        val_hi, val_lo = val[:, :, 0], val[:, :, 1]
        z = sb("z", [P, 2, N], F32)
        probs = sb("probs", [P, 2, N], F32)
        pT = sb("pT", [P, 2, 2, R, P], F16)
        pT_hi, pT_lo = pT[:, :, 0], pT[:, :, 1]
        s_j = sb("s_j", [P, 2, N], F32)
        s_i4 = sb("s_i4", [P, 2, R], F32)
        hw_hi = sb("hw_hi", [P, R, D + 1], F16)
        hw_lo = sb("hw_lo", [P, R, D], F16)
        hb = sb("hb", [P, R, D], F32)
        upd = sb("upd", [P, R, D], F32)
        type_mask = sb("type_mask", [P, N], I16)
        stats = sb("stats", [P, R, 6], F32)
        mean_var = sb("mean_var", [P, R, 2], F32)
        var_eps = sb("var_eps", [P, R], F32)
        rstd = sb("rstd", [P, R], F32)
        minus_half = sb("minus_half", [P, R], F32)
        row_max = sb("row_max", [P, 2, R], F32)
        top = sb("top", [P, 2], F32)
        exp_bias = sb("exp_bias", [P, 2], F32)
        row_sum = sb("row_sum", [P, 4], F32)
        row_inv = sb("row_inv", [P, 4], F32)
        degree = sb("degree", [P, 2], F32)
        degree_inv = sb("degree_inv", [P, 2], F32)
        m_hi = sb("m_hi", [P, TYPES, D], F16)
        m_lo = sb("m_lo", [P, TYPES, D], F16)
        m_bias = sb("m_bias", [P, TYPES], F32)
        kT_hi = sb("kT_hi", [P, D], F16)
        kT_lo = sb("kT_lo", [P, D], F16)
        v_hi = sb("v_hi", [P, D], F16)
        v_lo = sb("v_lo", [P, D], F16)
        wb_hi = sb("wb_hi", [P, 2 * D], F16)
        wb_lo = sb("wb_lo", [P, 2 * D], F16)
        w2_hi = sb("w2_hi", [P, D + 1], F16)
        w2_lo = sb("w2_lo", [P, D + 1], F16)
        wj_hi = sb("wj_hi", [P, P], F16)
        wj_lo = sb("wj_lo", [P, P], F16)
        v_bias = sb("v_bias", [P, D], F32)
        cols = sb("cols", [P, 5 + KINDS], F32)
        ident = sb("ident", [P, P], F32)
        ident_bf = sb("ident_bf", [P, P], BF16)
        ones = sb("ones", [P, P], F32)
        QB, KB, VB, AS, A3C = 0, 1, 2, 3, 5
        seen = sb("seen", [P, 1], F32)
        seen_now = sb("seen_now", [P, 1], F32)
        redo = sb("redo", [1, 1], I32)

        scores = ctx.enter_context(nc.psum_tensor("scores", [P, 4, HALF], F32))
        turned = ctx.enter_context(nc.psum_tensor("turned", [P, 2, HALF], F32))
        out_ps = ctx.enter_context(nc.psum_tensor("out_ps", [P, HALF], F32))
        head0 = ctx.enter_context(nc.psum_tensor("head", [P, HALF], F32))
        heads = [head0, scores[:, 3, :], scores[:, 2, :]][:HEADS]

        def whole(hi_lo, index):
            return hi_lo[:, index].rearrange("p h r i -> p (h r i)").bitcast(F32).rearrange("p (r i) -> p r i", r=R)

        adj_rows = adj.rearrange("b (r p) n -> b r p n", p=P)
        x_rows = x.rearrange("b (r p) d -> b p r d", p=P)
        out_rows = out.rearrange("b (r p) d -> b p r d", p=P)

        a_raw = z[:, 0, :]
        square = probs[:, :, :].rearrange("p a (m n) -> p (a m) n", n=D)
        QW, KW, VW, PW, W1R, B1R, W2R, PBR = range(8)
        square2 = z[:, 1, :].rearrange("p (m n) -> p m n", n=D)
        PWT, W2T, VBB, WJ = range(4)

        weights_in = sem("weights_in")
        ident_step = sem("ident_step")
        const_set = sem("const_set")
        fold_ready = sem("fold_ready")
        turn_w_ready = sem("turn_w_ready")
        turn_w_out = sem("turn_w_out")
        fold2_ready = sem("fold2_ready")
        wstep = sem("wstep")
        weights_done = sem("weights_done")
        with nc.Block() as block:
            @block.sync
            def _(sp):
                sp.dma_start(a_raw, a0.rearrange("d e t -> d (e t)")).then_inc(weights_in, 16)
                for k, w in ((QW, qw), (KW, kw), (VW, vw), (PW, pw), (W1R, W1), (B1R, B1), (W2R, W2)):
                    sp.dma_start(square[:, k, :], w).then_inc(weights_in, 16)
                sp.dma_start(square[:, PBR, :], pb.rearrange("(a d) -> a d", a=1).to_broadcast([P, D])
                             ).then_inc(weights_in, 16)
                for k, v in ((QB, qb), (KB, kb), (VB, vb)):
                    sp.dma_start(cols[:, k:k + 1], v.rearrange("(d a) -> d a", a=1)).then_inc(weights_in, 16)
                with nc.allow_non_contiguous_dma(reason="a few small columns"):
                    sp.dma_start(cols[:, AS:AS + 2], a2.rearrange("(a d) -> d a", a=2)).then_inc(weights_in, 16)
                    sp.dma_start(cols[:, A3C:A3C + KINDS], A3.rearrange("k d -> d k")).then_inc(weights_in, 16)

            LOADS = 14 * 16

            @block.gpsimd
            def _(pool):
                nc.gpsimd.memset(ident[:, :], 0.0).then_inc(ident_step, 1)
                pool.wait_ge(ident_step, 1)
                nc.gpsimd.affine_select(out=ident[:, :], in_=ident[:, :], compare_op=ALU.not_equal, fill=1.0,
                                        base=0, pattern=[[-1, P]], channel_multiplier=1).then_inc(ident_step, 1)
                pool.wait_ge(ident_step, 2)
                nc.gpsimd.tensor_copy(ident_bf[:, :], ident[:, :]).then_inc(const_set, 1)
                nc.gpsimd.memset(minus_half[:, :], -0.5).then_inc(const_set, 1)
                nc.gpsimd.memset(ones[:, :], 1.0).then_inc(const_set, 1)
                nc.gpsimd.memset(hw_hi[:, :, D:D + 1], 1.0).then_inc(const_set, 1)

            @block.tensor
            def _(pe):
                pe.wait_ge(weights_in, LOADS)
                for c in range(2):
                    nc.tensor.matmul(scores[:, c, :], square[:, QW, :], a_raw[:, c * HALF:(c + 1) * HALF],
                                     start=True, stop=True)
                for t in range(TYPES):
                    mm = nc.tensor.matmul(scores[:, 2, t:t + 1], a_raw.rearrange("p (e t) -> p t e", t=TYPES)[:, t, :],
                                          cols[:, QB:QB + 1], start=True, stop=True)
                mm.then_inc(fold_ready, 1)
                pe.wait_ge(ident_step, 2)
                for k, w in enumerate((KW, PW, W2R)):
                    mm = nc.tensor.transpose(scores[:, 3, k * D:(k + 1) * D], square[:, w, :], ident[:, :])
                mm.then_inc(turn_w_ready, 1)
                pe.wait_ge(turn_w_out, 1)
                nc.tensor.matmul(turned[:, 0, 0:D], square[:, VW, :], square2[:, PWT, :], start=True, stop=True)
                nc.tensor.matmul(turned[:, 1, 0:D], square2[:, VBB, :], square2[:, PWT, :], start=True, stop=True)
                nc.tensor.matmul(out_ps[:, 0:2], square2[:, W2T, :], cols[:, AS:AS + 2],
                                 start=True, stop=True).then_inc(fold2_ready, 1)

            @block.vector
            def _(dve):
                step = [0]

                def own(ins):
                    step[0] += 1
                    ins.then_inc(wstep, 1)
                    dve.wait_ge(wstep, step[0])

                def split(hi, lo, src):
                    own(nc.vector.tensor_copy(hi, src))
                    own(nc.vector.tensor_tensor(lo, src, hi, ALU.subtract))

                own(nc.vector.memset(seen[:, :], 0.0))
                dve.wait_ge(weights_in, LOADS)
                split(wb_hi[:, 0:D], wb_lo[:, 0:D], square[:, W1R, :])
                split(wb_hi[:, D:2 * D], wb_lo[:, D:2 * D], square[:, B1R, :])
                split(w2_hi[:, 0:D], w2_lo[:, 0:D], square[:, W2R, :])
                own(nc.vector.tensor_copy(square2[:, VBB, :], cols[:, VB:VB + 1].to_broadcast([P, D])))
                dve.wait_ge(fold_ready, 1)
                for c in range(2):
                    half = scores[:, c, :].rearrange("p (e t) -> p t e", t=TYPES)
                    split(m_hi[:, :, c * 64:(c + 1) * 64], m_lo[:, :, c * 64:(c + 1) * 64], half)
                own(nc.vector.tensor_copy(m_bias[:, :], scores[:, 2, 0:TYPES]))
                dve.wait_ge(turn_w_ready, 1)
                own(nc.vector.tensor_copy(square2[:, PWT, :], scores[:, 3, D:2 * D]))
                nc.vector.tensor_copy(square2[:, W2T, :], scores[:, 3, 2 * D:3 * D]).then_inc(turn_w_out, 1)
                split(kT_hi[:, :], kT_lo[:, :], scores[:, 3, 0:D])
                dve.wait_ge(fold2_ready, 1)
                split(v_hi[:, :], v_lo[:, :], turned[:, 0, 0:D])
                own(nc.vector.tensor_tensor(v_bias[:, :], turned[:, 1, 0:D], square[:, PBR, :], ALU.add))
                split(w2_hi[:, D:D + 1], w2_lo[:, D:D + 1], out_ps[:, 0:1])
                own(nc.vector.tensor_copy(square2[:, WJ, :], out_ps[:, 1:2].to_broadcast([P, D])))
                split(wj_hi[:, :], wj_lo[:, :], square2[:, WJ, :])

        def one_pass(block, all_types, when):
            tag = "all_" if all_types else ""
            slots = 1 if all_types else 2
            types = TYPES if all_types else 2
            kinds = KINDS if all_types else 1
            turns = B // slots
            order = schedule(all_types)
            ahead = [] if all_types else sorted((ev for ev in order if of_next_turn(ev)),
                                                key=lambda ev: {"fetch": 0, "code": 2}.get(ev[0], 1))
            order_of_last = [ev for ev in order if ev not in ahead]

            def over_turns(engine, run):
                with when(engine):
                    if ahead:
                        run(ahead, -1)
                    with engine.Fori(0, turns - 1 if ahead else turns) as turn:
                        run(order, turn)
                    if ahead:
                        run(order_of_last, turns - 1)

            tiles = slots * 3 * R
            halves0 = slots * R * 2
            picks0 = halves0 * (types - 1)
            tiles3 = slots * R * kinds
            bank_steps = [ev[1:] for ev in order if ev[0] == "light" and ev[1] in USES_BANK]
            hi_steps = [st for st in bank_steps if st[0] in USES_ACT and st[0] not in ("wh", "s_j")]
            norms = [ev[1:] for ev in order if ev[0] == "light" and ev[1] == "stats" and ev[4] == 0]
            banks_ahead = len([ev for ev in ahead if ev[0] == "light" and ev[1:] in bank_steps])
            beside, layer_now = {}, 0
            for ev in order:
                if ev[0] == "front0":
                    layer_now = ev[1]
                if ev[0] == "light":
                    beside[ev[1:]] = 0 if all_types else layer_now
            bank_of = [k % HEADS if beside[st] == 2 else 0 for k, st in enumerate(bank_steps)]
            his_ahead = len([ev for ev in ahead if ev[0] == "light" and ev[1:] in hi_steps])
            norms_ahead = len([ev for ev in ahead if ev[0] == "light" and ev[1:] in norms])
            tile_of = [ev[1:4] for ev in order if ev[0] == "bias"]

            split_tiles = [g for g, tile in enumerate(tile_of) if tile[0] != 2]
            first_whole = [tile[0] for tile in tile_of].index(2)

            def counted(name, per, start=0):
                return Count(sem(tag + name), per, start)

            x_in = [counted(f"x_in{s}", 16) for s in range(slots)]
            x_out = [counted(f"x_out{s}", 16) for s in range(slots)]
            stage_in = [counted(f"stage_in{q}", 16 * slots * R // STAGE) for q in range(STAGE)]
            code_done = counted("code_done", slots * R, start=1)
            code_used = [counted(f"code_used{s}", 1, start=1) for s in range(slots)]
            stats_done = counted("stats_done", len(norms), norms_ahead)
            rstd_done = counted("rstd_done", len(norms), norms_ahead)
            norm_done = counted("norm_done", 2 * len(norms), 2 * norms_ahead)
            head_ready = counted("head_ready", len(bank_steps), banks_ahead)
            head_hi = counted("head_hi", len(hi_steps), his_ahead)
            head_free = [counted(f"head_free{b}", bank_of.count(b),
                                 banks_ahead if b == 0 else 0) for b in range(HEADS)]
            x_pooled = counted("x_pooled", 2 * slots)
            picks_ready = counted("picks_ready", picks0)
            picked = counted("picked", picks0)
            relu0 = counted("relu0", halves0)
            leaky0 = counted("leaky0", halves0)
            sums_ready = counted("sums_ready", slots * R)
            relu2 = counted("relu2", slots * R)
            dots_ready = counted("dots_ready", tiles3)
            relu3 = counted("relu3", slots * R)
            dots_used = counted("dots_used", tiles3)
            bias_ready = counted("bias_ready", tiles)
            probs_ready = counted("probs_ready", tiles)
            turned_ready = counted("turned_ready", 2 * tiles)
            hi_ready = counted("hi_ready", 2 * len(split_tiles))
            lo_ready = counted("lo_ready", 2 * tiles)
            inv_ready = counted("inv_ready", tiles)
            out_ready = counted("out_ready", tiles)
            x_added = counted("x_added", tiles)
            unread = sem(tag + "unread")
            own_step = sem(tag + "dve_step")
            pool_step = counted("pool_step", len(norms), norms_ahead)

            def own_steps(ev):
                if ev[0] == ("late" if ev[1] in USES_BANK else "light"):
                    return {"stats": int(ev[4] == 1) + 2 * (ev[2] == 3 and ev[4] == 0 and not all_types),
                            "norm": int(ev[2] == 3 or (ev[2] == 0 and ev[4] == 1)), "pool": 2,
                            "update": 1, "mask": 1, "witness": 4 if ev[4] == 3 else 1,
                            "proj": int(all_types and ev[4] == 0)}.get(ev[1], 0)
                if ev[0] in ("front0", "front1") and ev[1] == 0:
                    return 6 + types - 1 if all_types else 0
                if ev[0] == "bias":
                    return {0: 0, 2: 1, 3: kinds + 3 if all_types else 0}[ev[1]]
                return 0

            own_per_turn = sum(own_steps(ev) for ev in order)
            own_ahead = sum(own_steps(ev) for ev in ahead)

            def last_tile(layer, s):
                return max(g for g, tile in enumerate(tile_of) if tile[:2] == (layer, s))

            def wait_read(engine, turn, k, banks=range(HEADS)):
                for b in banks:
                    done = bank_of[:k].count(b)
                    if done or (b == 0 and ahead):
                        engine.wait_ge(head_free[b].sem, head_free[b].at(turn, done))

            def bank_index(st):
                return bank_steps.index(st)

            def last_bank_step(layer, s):
                k = max(k for k, st in enumerate(bank_steps) if st[1] == layer and st[2] == s)
                return -1 if ("light",) + bank_steps[k] in ahead else k

            def src_row(s, t):
                return t if all_types else 2 * s + t

            def wait_apart(engine, sem, value):
                engine.wait_ge(sem, value)
                engine.sem_inc(unread, 1)

            def three(psum, lhs, rhs, start, stop):
                nc.tensor.matmul(psum, lhs[0], rhs[0], start=start, stop=False)
                nc.tensor.matmul(psum, lhs[0], rhs[1], start=False, stop=False)
                return nc.tensor.matmul(psum, lhs[1], rhs[0], start=False, stop=stop)


            @block.sync
            def _(sp):
                with when(sp), sp.Fori(0, turns) as turn:
                    for s in range(slots):
                        for r in range(R):
                            c = s * R + r
                            sp.wait_ge(code_done.sem, code_done.at(turn, s * R if r < STAGE else c - STAGE + 1))
                            sp.dma_start(stage[:, r % STAGE, :], adj_rows[turn * slots + s, r]
                                         ).then_inc(stage_in[r % STAGE].sem, 16)

            @block.gpsimd
            def _(pool):
                for count in (*code_used, code_done):
                    pool.sem_inc(count.sem, count.start)

                def run(events, turn):
                    for ev in events:
                        if ev[0] == "fetch":
                            s = ev[1]
                            later = 0 if all_types else 1
                            if later and events is not ahead:
                                pool.wait_ge(x_out[s].sem, x_out[s].at(turn, 16))
                            pool.dma_start(xs[:, s], x_rows[(turn + later) * slots + s]).then_inc(x_in[s].sem, 16)
                        elif ev[0] == "code":
                            _, s, r = ev
                            later = int(ev in ahead)
                            if r == 0 and not all_types:
                                pool.wait_ge(code_used[s].sem, code_used[s].at(turn, later))
                            ring = stage_in[r % STAGE]
                            wait_apart(pool, ring.sem, ring.at(turn, 16 * ((s + slots * later) * R // STAGE
                                                                           + r // STAGE + 1)))
                            nc.gpsimd.tensor_copy(code[:, s, r, :], stage[:, r % STAGE, :]
                                                  ).then_inc(code_done.sem, 1)
                        elif ev[0] == "light" and ev[1] == "rstd":
                            k = norms.index(("stats",) + ev[2:])
                            wait_apart(pool, stats_done.sem, stats_done.at(turn, k + 1))
                            nc.gpsimd.tensor_scalar(var_eps[:, :], mean_var[:, :, 1], EPS, None, ALU.add
                                                    ).then_inc(pool_step.sem, 1)
                            pool.wait_ge(pool_step.sem, pool_step.at(turn, k + 1))
                            nc.gpsimd.tensor_tensor(rstd[:, :], var_eps[:, :], minus_half[:, :], ALU.pow
                                                    ).then_inc(rstd_done.sem, 1)
                        elif ev[0] == "store":
                            s = ev[1]
                            wait_apart(pool, x_added.sem, x_added.at(turn, last_tile(3, s) + 1))
                            pool.dma_start(out_rows[turn * slots + s], xs[:, s]).then_inc(x_out[s].sem, 16)
                            if all_types:
                                pool.wait_ge(x_out[s].sem, x_out[s].at(turn, 16))

                over_turns(pool, run)
                if not all_types:
                    for s in range(slots):
                        pool.wait_ge(x_out[s].sem, x_out[s].at(turns - 1, 16))

            @block.tensor
            def _(pe):
                def run(events, turn):
                    for ev in events:
                        if ev[0] == "light" and ev[1] in USES_BANK:
                            _, kind, layer, s, c = ev
                            k = bank_index(ev[1:])
                            if events is not ahead or k > len(bank_steps) - banks_ahead:
                                needs_all = kind in ("dst", "proj", "pool", "wh") and c == 0
                                wait_read(pe, turn, k, range(HEADS) if needs_all else (bank_of[k],))
                            head = heads[bank_of[k]]
                            hT = (hT_hi[:, s, :], hT_lo[:, s, :])
                            if kind == "turn_h":
                                n = norms.index(("stats", layer, s, 0))
                                pe.wait_ge(norm_done.sem, norm_done.at(turn, 2 * n + c + 1))
                                for j in range(4):
                                    mm = nc.tensor.transpose(head[:, j * P:(j + 1) * P], hn[:, 4 * c + j, :],
                                                             ident[:, :])
                            elif kind in ("dst", "src", "s_j"):
                                t, c = divmod(c, 2)
                                w = {"dst": (kT_hi[:, :], kT_lo[:, :]), "src": (m_hi[:, t, :], m_lo[:, t, :]),
                                     "s_j": (wj_hi[:, :], wj_lo[:, :])}[kind]
                                ks = slice(c * HALF, (c + 1) * HALF)
                                mm = three(head[:, :], w, (hT[0][:, ks], hT[1][:, ks]), True, True)
                            elif kind in ("val", "proj", "wh"):
                                w, width, per = {"val": ((v_hi, v_lo), D, 4), "proj": ((wb_hi, wb_lo), 2 * D, 2),
                                                 "wh": ((w2_hi, w2_lo), D + 1, 3)}[kind]
                                for j in range(min(per, R - c * per)):
                                    ns = slice((c * per + j) * P, (c * per + j + 1) * P)
                                    mm = three(head[:, j * width:(j + 1) * width],
                                               (hT[0][:, ns], hT[1][:, ns]), (w[0][:, :], w[1][:, :]), True, True)
                            elif kind == "pool":
                                if c == 0 and not all_types:
                                    pe.wait_ge(code_done.sem, code_done.at(turn, (s + 1) * R))
                                edges = minus if all_types else code
                                for j in range(2):
                                    ns = slice((2 * c + j) * P, (2 * c + j + 1) * P)
                                    o = j * (D + 1)
                                    for r in range(R):
                                        e = (edges[:, s, r, ns].bitcast(F16) if all_types else edges[:, s, r, ns])
                                        hi = (head[:, o:o + D + 1], e, hw_hi[:, r, :])
                                        lo = (head[:, o:o + D], e, hw_lo[:, r, :])
                                        if r == 0:
                                            nc.tensor.matmul(*hi, start=True, stop=False)
                                            nc.tensor.matmul(*lo, start=False, stop=False)
                                        else:
                                            nc.tensor.matmul(*lo, start=False, stop=False)
                                            mm = nc.tensor.matmul(*hi, start=False, stop=(r == R - 1))
                            mm.then_inc(head_ready.sem, 1)

                        elif ev[0] in ("front0", "front1") and ev[1] == 0:
                            _, _, s, t, g = ev
                            hf = int(ev[0] == "front1")
                            h = 2 * (s * R + t) + hf
                            ks = slice(hf * HALF, (hf + 1) * HALF)
                            qs = slice(t * P, (t + 1) * P)
                            if t == 0 and hf == 0:
                                wait_read(pe, turn, last_bank_step(0, s) + 1)
                            for ty in range(types):
                                v = h * (types - 1) + ty - 1
                                if ty == 0 and h >= 2:
                                    pe.wait_ge(leaky0.sem, leaky0.at(turn, h - 1))
                                if ty >= 2:
                                    pe.wait_ge(picked.sem, picked.at(turn, v))
                                row = src_row(s, ty)
                                mm = three(scores[:, 2 * hf + min(ty, 1), :],
                                           (src_hi[:, row, qs], src_lo[:, row, qs]),
                                           (dst_hi[:, s, ks], dst_lo[:, s, ks]), True, True)
                                if ty:
                                    mm.then_inc(picks_ready.sem, 1)

                        elif ev[0] == "front0" and ev[1] == 3:
                            _, _, s, t, g = ev
                            if t == 0:
                                wait_read(pe, turn, last_bank_step(3, s) + 1)
                            qs = slice(t * P, (t + 1) * P)
                            for kd in range(kinds):
                                w = (s * R + t) * kinds + kd
                                if w >= 2:
                                    pe.wait_ge(dots_used.sem, dots_used.at(turn, w - 1))
                                row = src_row(s, kd)
                                for hf in range(2):
                                    ks = slice(hf * HALF, (hf + 1) * HALF)
                                    bank = scores[:, 2 * (w % 2) + hf, :]
                                    mm = three(bank, (src_hi[:, row, qs], src_lo[:, row, qs]),
                                               (hT_hi[:, s, ks], hT_lo[:, s, ks]), True, all_types)
                                    if not all_types:
                                        mm = nc.tensor.matmul(bank, ident_bf[:, :], minus[:, s, t, ks],
                                                              start=False, stop=True)
                                mm.then_inc(dots_ready.sem, 1)

                        elif ev[0] == "turn":
                            g = ev[1]
                            pe.wait_ge(probs_ready.sem, probs_ready.at(turn, g + 1))
                            for hf in range(2):
                                if g >= 1:
                                    ahead_of = 0 if g == first_whole else 1 - hf
                                    pe.wait_ge(lo_ready.sem, lo_ready.at(turn, 2 * g - ahead_of))
                                for j in range(4):
                                    c = 4 * hf + j
                                    mm = nc.tensor.transpose(turned[:, hf, j * P:(j + 1) * P],
                                                             probs[:, g % 2, c * P:(c + 1) * P], ident[:, :])
                                mm.then_inc(turned_ready.sem, 1)

                        elif ev[0] == "out":
                            _, layer, s, t, g = ev
                            pe.wait_ge(lo_ready.sem, lo_ready.at(turn, 2 * g + 2))
                            if g >= 1:
                                pe.wait_ge(x_added.sem, x_added.at(turn, g))
                            for c in range(R):
                                if layer == 2:
                                    mm = nc.tensor.matmul(out_ps[:, 0:D], whole(pT, g % 2)[:, c, :],
                                                          whole(val, s)[:, c, :], start=c == 0, stop=c == R - 1)
                                    continue
                                mm = three(out_ps[:, 0:D], (pT_hi[:, g % 2, c, :], pT_lo[:, g % 2, c, :]),
                                           (val_hi[:, s, c, :], val_lo[:, s, c, :]), c == 0, c == R - 1)
                            mm.then_inc(out_ready.sem, 1)

                over_turns(pe, run)

            @block.scalar
            def _(act):
                def run(events, turn):
                    for ev in events:
                        if ev[0] == "late" and ev[1] in USES_ACT:
                            _, kind, layer, s, c = ev
                            k = bank_index(ev[1:])
                            head = heads[bank_of[k]]
                            act.wait_ge(head_ready.sem, head_ready.at(turn, k + 1))
                            if kind == "turn_h":
                                ks = slice(c * HALF, (c + 1) * HALF)
                                ins = nc.scalar.activation(hT_hi[:, s, ks], head[:, :], ACT.Relu)
                                if layer == 3:
                                    for kd in range(kinds):
                                        nc.scalar.activation(src_hi[:, src_row(s, kd), ks], head[:, :], ACT.Identity,
                                                             scale=cols[:, A3C + kd:A3C + kd + 1])
                                    ins = nc.scalar.activation(
                                        val_hi[:, s, 4 * c:4 * c + 4, :], hn[:, 4 * c:4 * c + 4, :], ACT.Copy)
                            elif kind in ("dst", "src"):
                                t, c = divmod(c, 2)
                                ks = slice(c * HALF, (c + 1) * HALF)
                                if kind == "dst":
                                    ins = nc.scalar.activation(dst_hi[:, s, ks], head[:, :], ACT.Identity,
                                                               bias=cols[:, KB:KB + 1])
                                else:
                                    ins = nc.scalar.activation(src_hi[:, src_row(s, t), ks], head[:, :],
                                                               ACT.Identity, bias=m_bias[:, t:t + 1])
                            elif kind == "val":
                                ins = nc.scalar.activation(val_hi[:, s, 4 * c:4 * c + 4, :],
                                                           head[:, :].rearrange("p (j d) -> p j d", d=D), ACT.Copy)
                            elif kind == "proj":
                                two = head[:, :].rearrange("p (j d) -> p j d", d=2 * D)
                                nc.scalar.activation(hw_hi[:, 2 * c:2 * c + 2, 0:D], two[:, :, 0:D], ACT.Copy)
                                ins = nc.scalar.activation(hb[:, 2 * c:2 * c + 2, :], two[:, :, D:2 * D], ACT.Copy)
                            elif kind == "wh":
                                n = min(3, R - 3 * c)
                                rows = head[:, 0:n * (D + 1)].rearrange("p (j d) -> p j d", d=D + 1)
                                nc.scalar.activation(whole(val, s)[:, 3 * c:3 * c + n, :], rows[:, :, 0:D], ACT.Copy)
                                nc.scalar.activation(s_i4[:, s, 3 * c:3 * c + n], rows[:, :, D], ACT.Copy, scale=4.0
                                                     ).then_inc(head_free[bank_of[k]].sem, 1)
                                continue
                            elif kind == "s_j":
                                nc.scalar.activation(s_j[:, s, c * HALF:(c + 1) * HALF], head[:, :],
                                                     ACT.Copy).then_inc(head_free[bank_of[k]].sem, 1)
                                continue
                            ins.then_inc(head_hi.sem, 1)

                        elif ev[0] in ("front0", "front1") and ev[1] == 0:
                            _, _, s, t, g = ev
                            hf = int(ev[0] == "front1")
                            h = 2 * (s * R + t) + hf
                            act.wait_ge(picked.sem, picked.at(turn, (h + 1) * (types - 1)))
                            if hf == 0 and g >= 2:
                                act.wait_ge(turned_ready.sem, turned_ready.at(turn, 2 * g - 2))
                            nc.scalar.activation(probs[:, g % 2, hf * HALF:(hf + 1) * HALF], scores[:, 2 * hf, :],
                                                 ACT.Relu, scale=4.0).then_inc(relu0.sem, 1)

                        elif ev[0] == "front1" and ev[1] == 2:
                            _, _, s, t, g = ev
                            act.wait_ge(sums_ready.sem, sums_ready.at(turn, s * R + t + 1))
                            if g >= 2:
                                act.wait_ge(turned_ready.sem, turned_ready.at(turn, 2 * g - 2))
                            nc.scalar.activation(probs[:, g % 2, :], z[:, g % 2, :], ACT.Relu,
                                                 bias=s_i4[:, s, t:t + 1], scale=4.0).then_inc(relu2.sem, 1)

                        elif ev[0] == "front1" and ev[1] == 3 and not all_types:
                            _, _, s, t, g = ev
                            u = s * R + t
                            act.wait_ge(dots_ready.sem, dots_ready.at(turn, u + 1))
                            act.wait_ge(turned_ready.sem, turned_ready.at(turn, 2 * g - 2))
                            pair = scores[:, 2 * (u % 2):2 * (u % 2) + 2, :].rearrange("p a n -> p (a n)")
                            nc.scalar.activation(probs[:, g % 2, :], pair, ACT.Relu, scale=4.0
                                                 ).then_inc(relu3.sem, 1)

                        elif ev[0] == "exp":
                            g = ev[1]
                            act.wait_ge(bias_ready.sem, bias_ready.at(turn, g + 1))
                            if tile_of[g][0] == 3 and all_types:
                                act.wait_ge(turned_ready.sem, turned_ready.at(turn, 2 * g - 2))
                            nc.scalar.activation(probs[:, g % 2, :], z[:, g % 2, :], ACT.Exp,
                                                 bias=exp_bias[:, g % 2:g % 2 + 1],
                                                 accum_out=row_sum[:, g % 4:g % 4 + 1]).then_inc(probs_ready.sem, 1)

                        elif ev[0] == "turn":
                            g = ev[1]
                            if g >= 2:
                                act.wait_ge(out_ready.sem, out_ready.at(turn, g - 1))
                            for hf in range(2):
                                act.wait_ge(turned_ready.sem, turned_ready.at(turn, 2 * g + hf + 1))
                                if tile_of[g][0] == 2:
                                    nc.scalar.activation(whole(pT, g % 2)[:, 4 * hf:4 * hf + 4, :],
                                                         turned[:, hf, :].rearrange("p (j i) -> p j i", i=P),
                                                         ACT.Copy).then_inc(lo_ready.sem, 1)
                                    continue
                                nc.scalar.activation(pT_hi[:, g % 2, 4 * hf:4 * hf + 4, :],
                                                     turned[:, hf, :].rearrange("p (j i) -> p j i", i=P),
                                                     ACT.Copy).then_inc(hi_ready.sem, 1)

                over_turns(act, run)

            @block.vector
            def _(dve):
                own = [0]

                def run(events, turn):
                    own[0] = own_per_turn - own_ahead if events is ahead else 0

                    def settled(ins, apart=False):
                        own[0] += 1
                        ins.then_inc(own_step, 1)
                        value = turn * own_per_turn + own_ahead + own[0]
                        if apart:
                            wait_apart(dve, own_step, value)
                        else:
                            dve.wait_ge(own_step, value)

                    def pick_type(value, ks, s, t):
                        settled(nc.vector.tensor_scalar(type_mask[:, ks], code[:, s, t, ks], value, None,
                                                        ALU.is_equal), apart=True)

                    def leaky_half(turn, s, t, g, hf):
                        h = 2 * (s * R + t) + hf
                        ks = slice(hf * HALF, (hf + 1) * HALF)
                        mx = top[:, g % 2:g % 2 + 1]
                        if hf == 0 and g >= 2:
                            dve.wait_ge(probs_ready.sem, probs_ready.at(turn, g - 1))
                        if hf == 1:
                            dve.wait_ge(leaky0.sem, leaky0.at(turn, h))
                        wait_apart(dve, relu0.sem, relu0.at(turn, h + 1))
                        nc.vector.tensor_tensor_reduce(z[:, g % 2, ks], scores[:, 2 * hf, :], probs[:, g % 2, ks], 0.2,
                                                       mx if hf else LOWEST, ALU.add, ALU.max, mx
                                                       ).then_inc(leaky0.sem, 1)

                    for ev in events:
                        if ev[0] == ("late" if ev[1] in USES_BANK else "light"):
                            _, kind, layer, s, c = ev
                            n = norms.index(("stats", layer, s, 0))
                            if kind in USES_BANK:
                                k = bank_index(ev[1:])
                                head = heads[bank_of[k]]
                            if ev[1:] in hi_steps:
                                dve.wait_ge(head_hi.sem, head_hi.at(turn, hi_steps.index(ev[1:]) + 1))

                            half = range(4 * c, 4 * c + 4)
                            rows = slice(4 * c, 4 * c + 4)
                            if kind == "stats":
                                if c == 0 and layer == 0:
                                    dve.wait_ge(x_in[s].sem, x_in[s].at(turn, 32 if ev in ahead else 16))
                                elif c == 0 and layer == 2:
                                    dve.wait_ge(x_pooled.sem, x_pooled.at(turn, 2 * s + 2))
                                elif c == 0:
                                    dve.wait_ge(x_added.sem, x_added.at(turn, last_tile(layer - 1, s) + 1))
                                if c == 0 and layer == 3 and not all_types:
                                    settled(nc.vector.tensor_reduce(seen_now[:, :], row_max[:, s, :], AX.X,
                                                                    ALU.min))
                                    settled(nc.vector.scalar_tensor_tensor(seen[:, :], seen_now[:, :], 0.5 * MASKED,
                                                                           seen[:, :], ALU.is_lt, ALU.max))
                                for r in half:
                                    ins = nc.vector.bn_stats(stats[:, r, :], xs[:, s, r, :])
                                if c == 1:
                                    settled(ins, apart=True)
                                    for r in range(R):
                                        ins = nc.vector.bn_aggr(mean_var[:, r, :], stats[:, r, :])
                                    ins.then_inc(stats_done.sem, 1)
                            elif kind == "norm":
                                dve.wait_ge(rstd_done.sem, rstd_done.at(turn, n + 1))
                                for r in half:
                                    ins = nc.vector.tensor_scalar(hn[:, r, :], xs[:, s, r, :], mean_var[:, r, 0:1],
                                                                  rstd[:, r:r + 1], ALU.subtract, ALU.mult)
                                if layer == 3:
                                    settled(ins)
                                    ins = nc.vector.tensor_scalar(hn[:, rows, :], hn[:, rows, :], 0.0, None, ALU.max)
                                ins.then_inc(norm_done.sem, 1)
                                if layer == 0 and c == 1:
                                    dve.wait_ge(norm_done.sem, norm_done.at(turn, 2 * n + 2))
                                    settled(nc.vector.tensor_tensor(
                                        xs[:, s], xs[:, s], v_bias[:, None, :].to_broadcast([P, R, D]), ALU.add))
                            elif kind == "turn_h":
                                ks = slice(c * HALF, (c + 1) * HALF)
                                ins = nc.vector.scalar_tensor_tensor(hT_lo[:, s, ks], head[:, :], 0.0,
                                                                     hT_hi[:, s, ks], ALU.max, ALU.subtract)
                                if layer == 3:
                                    for kd in range(kinds):
                                        row = src_row(s, kd)
                                        nc.vector.scalar_tensor_tensor(
                                            src_lo[:, row, ks], head[:, :], cols[:, A3C + kd:A3C + kd + 1],
                                            src_hi[:, row, ks], ALU.mult, ALU.subtract)
                                    rs = slice(4 * c, 4 * c + 4)
                                    ins = nc.vector.tensor_tensor(val_lo[:, s, rs, :], hn[:, rs, :],
                                                                  val_hi[:, s, rs, :], ALU.subtract)
                                ins.then_inc(head_free[bank_of[k]].sem, 1)
                            elif kind == "dst":
                                ks = slice(c * HALF, (c + 1) * HALF)
                                nc.vector.scalar_tensor_tensor(dst_lo[:, s, ks], head[:, :], cols[:, KB:KB + 1],
                                                               dst_hi[:, s, ks], ALU.add, ALU.subtract
                                                               ).then_inc(head_free[bank_of[k]].sem, 1)
                            elif kind == "src":
                                t, c = divmod(c, 2)
                                ks = slice(c * HALF, (c + 1) * HALF)
                                row = src_row(s, t)
                                nc.vector.scalar_tensor_tensor(src_lo[:, row, ks], head[:, :], m_bias[:, t:t + 1],
                                                               src_hi[:, row, ks], ALU.add, ALU.subtract
                                                               ).then_inc(head_free[bank_of[k]].sem, 1)
                            elif kind == "val":
                                rs = slice(4 * c, 4 * c + 4)
                                nc.vector.tensor_tensor(val_lo[:, s, rs, :],
                                                        head[:, :].rearrange("p (j d) -> p j d", d=D),
                                                        val_hi[:, s, rs, :], ALU.subtract
                                                        ).then_inc(head_free[bank_of[k]].sem, 1)
                            elif kind == "proj":
                                if c == 0 and all_types:
                                    dve.wait_ge(code_done.sem, code_done.at(turn, (s + 1) * R))
                                    settled(nc.vector.tensor_scalar(minus[:, s].bitcast(F16), code[:, s], 0.0, None,
                                                                    ALU.not_equal))
                                two = head[:, :].rearrange("p (j d) -> p j d", d=2 * D)
                                nc.vector.tensor_tensor(hw_lo[:, 2 * c:2 * c + 2, :], two[:, :, 0:D],
                                                        hw_hi[:, 2 * c:2 * c + 2, 0:D], ALU.subtract
                                                        ).then_inc(head_free[bank_of[k]].sem, 1)
                            elif kind == "pool":
                                two = head[:, 0:2 * (D + 1)].rearrange("p (j d) -> p j d", d=D + 1)
                                dve.wait_ge(head_ready.sem, head_ready.at(turn, k + 1))
                                settled(nc.vector.tensor_scalar(degree[:, :], two[:, :, D], 1.0, None, ALU.max))
                                settled(nc.vector.reciprocal(degree_inv[:, :], degree[:, :]))
                                for j in range(2):
                                    ins = nc.vector.scalar_tensor_tensor(
                                        upd[:, 2 * c + j, :], two[:, j, 0:D], degree_inv[:, j:j + 1],
                                        hb[:, 2 * c + j, :], ALU.mult, ALU.add)
                                ins.then_inc(head_free[bank_of[k]].sem, 1)
                            elif kind == "update":
                                wait_read(dve, turn, last_bank_step(1, s) + 1)
                                settled(nc.vector.scalar_tensor_tensor(upd[:, rows, :], upd[:, rows, :], 0.1,
                                                                       upd[:, rows, :], ALU.mult, ALU.max))
                                nc.vector.tensor_tensor(xs[:, s, rows, :], xs[:, s, rows, :], upd[:, rows, :], ALU.add
                                                        ).then_inc(x_pooled.sem, 1)
                            elif kind == "witness":
                                word = [code[:, s, 2 * q:2 * q + 2, :].rearrange("p r n -> p (r n)").bitcast(I32)
                                        for q in range(4)]
                                a, b = (src_hi[:, q:q + 2, :].rearrange("p r n -> p (r n)").bitcast(I32)
                                        for q in (4, 6))
                                if c == 0:
                                    dve.wait_ge(code_done.sem, code_done.at(turn, (s + 1) * R))
                                    settled(nc.vector.tensor_tensor(a, word[0], word[1], ALU.bitwise_or))
                                elif c == 1:
                                    settled(nc.vector.tensor_tensor(b, word[2], word[3], ALU.bitwise_or))
                                elif c == 2:
                                    settled(nc.vector.tensor_tensor(a, a, b, ALU.bitwise_or))
                                else:
                                    settled(nc.vector.tensor_tensor(b[:, 0:512], a[:, 0:512], a[:, 512:1024],
                                                                    ALU.bitwise_or))
                                    settled(nc.vector.tensor_tensor(a[:, 0:256], b[:, 0:256], b[:, 256:512],
                                                                    ALU.bitwise_or))
                                    settled(nc.vector.tensor_reduce(seen_now[:, :], a[:, 0:256].bitcast(U16), AX.X,
                                                                    ALU.max))
                                    settled(nc.vector.scalar_tensor_tensor(seen[:, :], seen_now[:, :], float(BITS_OF_1),
                                                                           seen[:, :], ALU.is_gt, ALU.max))
                            elif kind == "mask":
                                rs = slice(2 * c, 2 * c + 2)
                                if c == 0:
                                    dve.wait_ge(code_done.sem, code_done.at(turn, (s + 1) * R))
                                settled(nc.vector.tensor_scalar(minus[:, s, rs], code[:, s, rs], 0.0, MASKED,
                                                                ALU.is_equal, ALU.mult))
                                if c == 3:
                                    nc.vector.tensor_copy(degree[:, 0:1], degree_inv[:, 0:1]
                                                          ).then_inc(code_used[s].sem, 1)

                        elif ev[0] in ("front0", "front1") and ev[1] == 0:
                            _, _, s, t, g = ev
                            hf = int(ev[0] == "front1")
                            h = 2 * (s * R + t) + hf
                            ks = slice(hf * HALF, (hf + 1) * HALF)
                            if t == 0 and hf == 0:
                                dve.wait_ge(code_done.sem, code_done.at(turn, (s + 1) * R))
                            for ty in range(1, types):
                                v = h * (types - 1) + ty - 1
                                wait_apart(dve, picks_ready.sem, picks_ready.at(turn, v + 1))
                                base = scores[:, 2 * hf, :]
                                if not all_types:
                                    mask = code[:, s, t, ks].bitcast(I16)
                                else:
                                    if ty == 1:
                                        for op, bound, fill in ((ALU.is_equal, -1.0, MASKED),
                                                                (ALU.is_gt, TYPES - 1.0, -LOWEST)):
                                            settled(nc.vector.tensor_scalar(type_mask[:, ks], code[:, s, t, ks],
                                                                            bound, None, op))
                                            settled(nc.vector.memset(s_j[:, 0, ks], fill), apart=True)
                                            settled(nc.vector.copy_predicated(base, type_mask[:, ks],
                                                                              s_j[:, 0, ks]))
                                    pick_type(float(ty), ks, s, t)
                                    mask = type_mask[:, ks]
                                nc.vector.copy_predicated(base, mask, scores[:, 2 * hf + 1, :]
                                                          ).then_inc(picked.sem, 1)
                                if all_types:
                                    dve.wait_ge(picked.sem, picked.at(turn, v + 1))
                            if hf == 1:
                                leaky_half(turn, s, t, g, 0)

                        elif ev[0] == "front0" and ev[1] == 2:
                            _, _, s, t, g = ev
                            if t == 0:
                                wait_read(dve, turn, last_bank_step(2, s) + 1)
                            wait_apart(dve, probs_ready.sem, probs_ready.at(turn, g - 1))
                            nc.vector.tensor_tensor_reduce(z[:, g % 2, :], s_j[:, s, :], minus[:, s, t, :], 1.0, LOWEST,
                                                           ALU.add, ALU.max, row_max[:, s, t:t + 1]
                                                           ).then_inc(sums_ready.sem, 1)

                        elif ev[0] == "bias":
                            _, layer, s, t, g = ev
                            u = s * R + t
                            zt, relu, mx = z[:, g % 2, :], probs[:, g % 2, :], top[:, g % 2:g % 2 + 1]
                            eb = exp_bias[:, g % 2:g % 2 + 1]
                            if layer == 0:
                                leaky_half(turn, s, t, g, 1)
                                dve.wait_ge(leaky0.sem, leaky0.at(turn, 2 * u + 2))
                                nc.vector.tensor_scalar(eb, mx, -1024.0, 1.0 / 1024, ALU.mult, ALU.mult
                                                        ).then_inc(bias_ready.sem, 1)
                            elif layer == 2:
                                wait_apart(dve, relu2.sem, relu2.at(turn, u + 1))
                                settled(nc.vector.tensor_tensor_reduce(zt, zt, relu, 0.2, LOWEST, ALU.add, ALU.max, mx))
                                nc.vector.tensor_scalar(eb, mx, -1024.0, 1.0 / 1024, ALU.mult, ALU.mult
                                                        ).then_inc(bias_ready.sem, 1)
                            else:
                                dve.wait_ge(probs_ready.sem, probs_ready.at(turn, g - 1))
                                if not all_types:
                                    wait_apart(dve, relu3.sem, relu3.at(turn, u + 1))
                                    pair = scores[:, 2 * (u % 2):2 * (u % 2) + 2, :].rearrange("p a n -> p (a n)")
                                    nc.vector.tensor_tensor_reduce(zt, pair, relu, 0.2, LOWEST, ALU.add, ALU.max, mx
                                                                   ).then_inc(dots_used.sem, 1)
                                    dve.wait_ge(dots_used.sem, dots_used.at(turn, u + 1))
                                    nc.vector.tensor_scalar(eb, mx, -1.0, None, ALU.mult
                                                            ).then_inc(bias_ready.sem, 1)
                                else:
                                    settled(nc.vector.memset(zt, LAYER3_NONE))
                                    for kd in range(kinds):
                                        w = u * kinds + kd
                                        dve.wait_ge(dots_ready.sem, dots_ready.at(turn, w + 1))
                                        pair = scores[:, 2 * (w % 2):2 * (w % 2) + 2, :].rearrange("p a n -> p (a n)")
                                        pick_type(kd + 1.0, slice(0, N), s, t)
                                        nc.vector.copy_predicated(zt, type_mask[:, :], pair
                                                                  ).then_inc(dots_used.sem, 1)
                                        dve.wait_ge(dots_used.sem, dots_used.at(turn, w + 1))
                                    settled(nc.vector.scalar_tensor_tensor(zt, zt, 0.2, zt, ALU.mult, ALU.max))
                                    settled(nc.vector.tensor_reduce(mx, zt, AX.X, ALU.max))
                                    nc.vector.tensor_scalar(eb, mx, -1.0, None, ALU.mult
                                                            ).then_inc(bias_ready.sem, 1)

                        elif ev[0] == "turn":
                            g = ev[1]
                            for hf in range(2 if g in split_tiles else 0):
                                v = 2 * split_tiles.index(g) + hf
                                dve.wait_ge(hi_ready.sem, hi_ready.at(turn, v + 1))
                                nc.vector.tensor_tensor(pT_lo[:, g % 2, 4 * hf:4 * hf + 4, :],
                                                        turned[:, hf, :].rearrange("p (j i) -> p j i", i=P),
                                                        pT_hi[:, g % 2, 4 * hf:4 * hf + 4, :], ALU.subtract
                                                        ).then_inc(lo_ready.sem, 1)
                            if g not in split_tiles:
                                dve.wait_ge(probs_ready.sem, probs_ready.at(turn, g + 1))
                            nc.vector.reciprocal(row_inv[:, g % 4:g % 4 + 1], row_sum[:, g % 4:g % 4 + 1]
                                                 ).then_inc(inv_ready.sem, 1)

                        elif ev[0] == "out":
                            _, layer, s, t, g = ev
                            dve.wait_ge(out_ready.sem, out_ready.at(turn, g + 1))
                            dve.wait_ge(inv_ready.sem, inv_ready.at(turn, g + 1))
                            nc.vector.scalar_tensor_tensor(xs[:, s, t, :], out_ps[:, 0:D],
                                                           row_inv[:, g % 4:g % 4 + 1], xs[:, s, t, :],
                                                           ALU.mult, ALU.add).then_inc(x_added.sem, 1)
                    assert own[0] == own_per_turn - (own_ahead if events is order_of_last and ahead else 0)

                over_turns(dve, run)

        with nc.Block() as block:
            one_pass(block, False, lambda engine: nullcontext())

        witness_sum = sem("witness_sum")
        redo_ready = sem("redo_ready")
        with nc.Block() as block:
            @block.vector
            def _(dve):
                dve.wait_ge(witness_sum, 1)
                nc.vector.tensor_copy(redo[:, :], head0[0:1, 0:1]).then_inc(redo_ready, 1)

            @block.tensor
            def _(pe):
                nc.tensor.matmul(head0[0:1, 0:1], seen[:, 0:1], ones[:, 0:1], start=True, stop=True
                                 ).then_inc(witness_sum, 1)

        @contextmanager
        def if_seen(engine):
            engine.wait_ge(redo_ready, 1)
            with engine.If(engine.value_load(redo[0:1, 0:1]) != 0):
                yield

        with nc.Block() as block:
            one_pass(block, True, if_seen)


_INS = ["x", "adj", "L0_gnn_a", "L0_gnn_qw", "L0_gnn_qb", "L0_gnn_kw", "L0_gnn_kb", "L0_gnn_vw", "L0_gnn_vb",
        "L0_gnn_pw", "L0_gnn_pb", "L1_gnn_W", "L1_gnn_B", "L2_gnn_W", "L2_gnn_a", "L3_gnn_A"]


def kernel(**inputs):
    import numpy as _np
    import concourse.bacc as _bacc
    from concourse import mybir as _mybir
    from concourse.bass_utils import run_bass_kernel_spmd as _run

    nc = _bacc.Bacc("TRN2", target_bir_lowering=False, num_devices=1)
    arrays, args = {}, []
    for name in _INS:
        a = _np.ascontiguousarray(inputs[name])
        arrays[f"in_{name}"] = a
        args.append(nc.dram_tensor(f"in_{name}", a.shape, _mybir.dt.from_np(a.dtype), kind="ExternalInput").ap())
    args.append(nc.dram_tensor("out_x", (B, N, D), _mybir.dt.float32, kind="ExternalOutput").ap())
    four_graph_layers_kernel(nc, *args)
    r = _run(nc, [arrays], core_ids=[0])
    return r.results[0]["out_x"]
```
